# Optimizing a Trainium2 kernel written in Bass

```python
import numpy as np
import jax
import jax.numpy as jnp

def _softmax(x, axis=-1):
    return jax.nn.softmax(x, axis=axis)

def _gelu(x):
    return jax.nn.gelu(x, approximate=True)

def _silu(x):
    return jax.nn.silu(x)

def _sigmoid(x):
    return jax.nn.sigmoid(x)

def _layernorm(x, axis=-1, eps=1e-05):
    m = jnp.mean(x, axis=axis, keepdims=True)
    v = jnp.var(x, axis=axis, keepdims=True)
    return (x - m) / jnp.sqrt(v + eps)

def _scatter_add(tgt, idx, src, axis=0):
    return tgt.at[idx].add(src)

def _segment_sum(src, seg, n):
    return jax.ops.segment_sum(src, seg, n)
kernel_name = 'mk_perceiver_d2_seqx_r8_324f2e'

def setup_inputs(seed: int=0):
    np.random.seed(seed)
    _w = jnp.asarray

    def _rec_inputs():
        import jax
        import jax.numpy as jnp
        _rk = jax.random.key(seed)
        x = 7.22e-05 + 1 * jax.random.normal(jax.random.fold_in(_rk, 1), (8, 32, 128), jnp.float32)
        _lenS = 32 - jax.random.randint(jax.random.fold_in(_rk, 7), (8,), 0, max(1, 32 // 4) + 1, jnp.int32)
        _lenS2 = 512 - jax.random.randint(jax.random.fold_in(_rk, 8), (8,), 0, max(1, 512 // 4) + 1, jnp.int32)
        _ctx_1024P = jax.random.normal(jax.random.fold_in(_rk, 11), (8, 16, 128), jnp.float32)
        _ctx_1024c = jax.random.dirichlet(jax.random.fold_in(_rk, 511), 0.3 * jnp.ones((16,), jnp.float32), (8, 512))
        _ctx_1024t = jnp.einsum('bsk,bkd->bsd', _ctx_1024c, _ctx_1024P)
        _ctx_1024t = _ctx_1024t * jax.lax.rsqrt(jnp.mean(jnp.square(_ctx_1024t)) + 1e-12) * 0.953939
        ctx_1024 = 4.13588e-05 + 0.999923 * (_ctx_1024t + 0.3 * jax.random.normal(jax.random.fold_in(_rk, 611), (8, 512, 128), jnp.float32))
        _validS = jnp.arange(32)[None, :] < _lenS[:, None]
        _validS2 = jnp.arange(512)[None, :] < _lenS2[:, None]
        _causal = jnp.tril(jnp.ones((32, 32), dtype=bool))
        mask_BxS2_bk0 = jnp.logical_not(jnp.broadcast_to(_validS2[:, :], (8, 512)))
        return (x, ctx_1024, mask_BxS2_bk0)
    x, ctx_1024, mask_BxS2_bk0 = _rec_inputs()

    def _L0_xattn_setup():
        import jax, jax.numpy as jnp
        import numpy as np
        H = 16
        D_MODEL = 128
        D_K = D_MODEL // H

        def _split_heads(x, B, T):
            return x.reshape(B, T, H, D_K).transpose(0, 2, 1, 3)
        key = jax.random.key(seed)
        ks = jax.random.split(key, 11)
        B, T = (4, 256)
        s = 1.0 / np.sqrt(D_MODEL)
        inp = {'query': jax.random.normal(ks[0], (B, T, D_MODEL), jnp.float32), 'key': jax.random.normal(ks[1], (B, T, D_MODEL), jnp.float32), 'value': jax.random.normal(ks[2], (B, T, D_MODEL), jnp.float32), 'Wq': jax.random.normal(ks[3], (D_MODEL, D_MODEL), jnp.float32) * s, 'bq': jnp.zeros((D_MODEL,), jnp.float32), 'Wk': jax.random.normal(ks[4], (D_MODEL, D_MODEL), jnp.float32) * s, 'bk': jnp.zeros((D_MODEL,), jnp.float32), 'Wv': jax.random.normal(ks[5], (D_MODEL, D_MODEL), jnp.float32) * s, 'bv': jnp.zeros((D_MODEL,), jnp.float32), 'Wo': jax.random.normal(ks[6], (D_MODEL, D_MODEL), jnp.float32) * s, 'bo': jnp.zeros((D_MODEL,), jnp.float32)}
        return inp
    _L0_xattn_all = _L0_xattn_setup()
    _L0_xattn_in = {k: v for k, v in _L0_xattn_all.items() if k in ('Wq', 'bq', 'Wk', 'bk', 'Wv', 'bv', 'Wo', 'bo')}
    del _L0_xattn_all

    def _L0_attn_setup():
        import jax, jax.numpy as jnp
        import numpy as np
        D_MODEL = 128
        NUM_HEADS = 16
        D_HEAD = D_MODEL // NUM_HEADS
        LAMBDA_INIT = 0.8
        EPS = 1e-05
        key = jax.random.key(seed)
        ks = jax.random.split(key, 10)
        B, N = (2, 256)

        def xav(k, shape):
            fan_in, fan_out = (shape[0], shape[1])
            lim = np.sqrt(6.0 / (fan_in + fan_out))
            return jax.random.uniform(k, shape, jnp.float32, -lim, lim)
        return {'X': jax.random.normal(ks[0], (B, N, D_MODEL), jnp.float32), 'Wq': xav(ks[1], (D_MODEL, 2 * D_MODEL)), 'Wk': xav(ks[2], (D_MODEL, 2 * D_MODEL)), 'Wv': xav(ks[3], (D_MODEL, 2 * D_MODEL)), 'Wo': xav(ks[4], (2 * D_MODEL, D_MODEL)), 'lambda_q1': jax.random.normal(ks[5], (NUM_HEADS, D_HEAD), jnp.float32), 'lambda_k1': jax.random.normal(ks[6], (NUM_HEADS, D_HEAD), jnp.float32), 'lambda_q2': jax.random.normal(ks[7], (NUM_HEADS, D_HEAD), jnp.float32), 'lambda_k2': jax.random.normal(ks[8], (NUM_HEADS, D_HEAD), jnp.float32), 'rms_scale': jnp.ones((2 * D_HEAD,), jnp.float32)}
    _L0_attn_all = _L0_attn_setup()
    _L0_attn_in = {k: v for k, v in _L0_attn_all.items() if k in ('Wq', 'Wk', 'Wv', 'Wo', 'lambda_q1', 'lambda_k1', 'lambda_q2', 'lambda_k2', 'rms_scale')}
    del _L0_attn_all

    def _L0_ffn_setup():
        import jax, jax.numpy as jnp
        import numpy as np
        E = 8
        TOP_K = 2
        ROUTE_SCALE = 1.0
        ALPHA = 1.702
        LIMIT = 7.0
        D = 128
        F = 128
        B, S = (2, 128)

        def swiglu(h):
            g = jnp.minimum(h[..., ::2], LIMIT)
            l = jnp.clip(h[..., 1::2], -LIMIT, LIMIT)
            return g * jax.nn.sigmoid(ALPHA * g) * (l + 1.0)
        if __name__ == '__main__':
            out = reference(**setup_inputs())
            print(out.shape, out.dtype)
        key = jax.random.key(seed)
        ks = jax.random.split(key, 16)
        sd = 1.0 / np.sqrt(D)
        sf = 1.0 / np.sqrt(F)
        return {'x': jax.random.normal(ks[0], (B, S, D), jnp.float32), 'gate_w': jax.random.normal(ks[1], (E, D), jnp.float32) * sd, 'gate_b': jax.random.normal(ks[2], (E,), jnp.float32) * 0.01, 'w1': jax.random.normal(ks[3], (E, 2 * F, D), jnp.float32) * sd, 'b1': jax.random.normal(ks[4], (E, 2 * F), jnp.float32) * 0.01, 'w3': jax.random.normal(ks[5], (E, 2 * F, D), jnp.float32) * sd, 'b3': jax.random.normal(ks[6], (E, 2 * F), jnp.float32) * 0.01, 'w2': jax.random.normal(ks[7], (E, D, F), jnp.float32) * sf, 'b2': jax.random.normal(ks[8], (E, D), jnp.float32) * 0.01, 'sw1': jax.random.normal(ks[9], (2 * F, D), jnp.float32) * sd, 'sb1': jax.random.normal(ks[10], (2 * F,), jnp.float32) * 0.01, 'sw3': jax.random.normal(ks[11], (2 * F, D), jnp.float32) * sd, 'sb3': jax.random.normal(ks[12], (2 * F,), jnp.float32) * 0.01, 'sw2': jax.random.normal(ks[13], (D, F), jnp.float32) * sf, 'sb2': jax.random.normal(ks[14], (D,), jnp.float32) * 0.01}
    _L0_ffn_all = _L0_ffn_setup()
    _L0_ffn_in = {k: v for k, v in _L0_ffn_all.items() if k in ('gate_w', 'gate_b', 'w1', 'b1', 'w3', 'b3', 'w2', 'b2', 'sw1', 'sb1', 'sw3', 'sb3', 'sw2', 'sb2')}
    del _L0_ffn_all

    def _L1_xattn_setup():
        import jax, jax.numpy as jnp
        import numpy as np
        DIM = 128
        DIM_HEAD = 64
        NUM_HEADS = 16
        HIDDEN = DIM_HEAD * NUM_HEADS
        EPS = 1e-05

        def layer_norm(t, gamma, beta):
            mu = jnp.mean(t, axis=-1, keepdims=True)
            var = jnp.var(t, axis=-1, keepdims=True)
            return (t - mu) * jax.lax.rsqrt(var + EPS) * gamma + beta
        key = jax.random.key(seed)
        ks = jax.random.split(key, 12)
        B, F, Q = (8, 512, 64)
        x = jax.random.normal(ks[0], (B, F, DIM), dtype=jnp.float32)
        latents = jax.random.normal(ks[1], (B, Q, DIM), dtype=jnp.float32)
        mask = jax.random.randint(ks[2], (B, F), 0, 2) == 1
        s = 1.0 / np.sqrt(DIM)
        Wq = jax.random.normal(ks[3], (DIM, HIDDEN), dtype=jnp.float32) * s
        Wkv = jax.random.normal(ks[4], (DIM, 2 * HIDDEN), dtype=jnp.float32) * s
        Wout = jax.random.normal(ks[5], (HIDDEN, DIM), dtype=jnp.float32) * (1.0 / np.sqrt(HIDDEN))
        bout = jnp.zeros((DIM,), dtype=jnp.float32)
        g_media = jnp.ones((DIM,), dtype=jnp.float32)
        b_media = jnp.zeros((DIM,), dtype=jnp.float32)
        g_latent = jnp.ones((DIM,), dtype=jnp.float32)
        b_latent = jnp.zeros((DIM,), dtype=jnp.float32)
        return {'x': x, 'latents': latents, 'mask': mask, 'Wq': Wq, 'Wkv': Wkv, 'Wout': Wout, 'bout': bout, 'g_media': g_media, 'b_media': b_media, 'g_latent': g_latent, 'b_latent': b_latent}
    _L1_xattn_all = _L1_xattn_setup()
    _L1_xattn_in = {k: v for k, v in _L1_xattn_all.items() if k in ('Wq', 'Wkv', 'Wout', 'bout', 'g_media', 'b_media', 'g_latent', 'b_latent')}
    del _L1_xattn_all

    def _L1_attn_setup():
        import jax, jax.numpy as jnp
        import numpy as np
        D_MODEL = 128
        RANK = 32
        INIT_ALPHA = 0.5
        key = jax.random.key(seed)
        ks = jax.random.split(key, 12)
        D, R = (D_MODEL, RANK)
        s = 0.02
        return {'x': jax.random.normal(ks[0], (4, 256, D), dtype=jnp.float32), 'Wq': jax.random.normal(ks[1], (D, D), dtype=jnp.float32) * s, 'Wk': jax.random.normal(ks[2], (D, D), dtype=jnp.float32) * s, 'Wo': jax.random.normal(ks[3], (D, D), dtype=jnp.float32) * s, 'U_b': jax.random.normal(ks[4], (D, R), dtype=jnp.float32) * s, 'V_b': jax.random.normal(ks[5], (D, R), dtype=jnp.float32) * s, 'W_b': jax.random.normal(ks[6], (D, R), dtype=jnp.float32) * s, 'bias_b': jnp.zeros((D,), dtype=jnp.float32), 'U_t': jax.random.normal(ks[7], (D, R), dtype=jnp.float32) * s, 'V_t': jax.random.normal(ks[8], (D, R), dtype=jnp.float32) * s, 'W_t': jax.random.normal(ks[9], (D, R), dtype=jnp.float32) * s, 'X_t': jax.random.normal(ks[10], (D, R), dtype=jnp.float32) * s, 'bias_t': jnp.zeros((D,), dtype=jnp.float32), 'alpha': jnp.asarray(INIT_ALPHA, dtype=jnp.float32)}
    _L1_attn_all = _L1_attn_setup()
    _L1_attn_in = {k: v for k, v in _L1_attn_all.items() if k in ('Wq', 'Wk', 'Wo', 'U_b', 'V_b', 'W_b', 'bias_b', 'U_t', 'V_t', 'W_t', 'X_t', 'bias_t', 'alpha')}
    del _L1_attn_all

    def _L1_ffn_setup():
        import jax, jax.numpy as jnp
        import numpy as np
        D_MODEL = 128
        NUM_EXPERTS = 8
        HIDDEN = 512
        TOP_K = 2
        key = jax.random.key(seed)
        ks = jax.random.split(key, 6)
        x = jax.random.normal(ks[0], (2, 128, D_MODEL), dtype=jnp.float32)
        gate_w = jax.random.normal(ks[1], (NUM_EXPERTS, D_MODEL), dtype=jnp.float32) * (1.0 / np.sqrt(D_MODEL))
        w1 = jax.random.normal(ks[2], (NUM_EXPERTS, HIDDEN, D_MODEL), dtype=jnp.float32) * (1.0 / np.sqrt(D_MODEL))
        b1 = jax.random.normal(ks[3], (NUM_EXPERTS, HIDDEN), dtype=jnp.float32) * 0.01
        w2 = jax.random.normal(ks[4], (NUM_EXPERTS, D_MODEL, HIDDEN), dtype=jnp.float32) * (1.0 / np.sqrt(HIDDEN))
        b2 = jax.random.normal(ks[5], (NUM_EXPERTS, D_MODEL), dtype=jnp.float32) * 0.01
        return {'x': x, 'gate_w': gate_w, 'w1': w1, 'b1': b1, 'w2': w2, 'b2': b2}
    _L1_ffn_all = _L1_ffn_setup()
    _L1_ffn_in = {k: v for k, v in _L1_ffn_all.items() if k in ('gate_w', 'w1', 'b1', 'w2', 'b2')}
    del _L1_ffn_all
    return {'x': x, 'ctx_1024': ctx_1024, 'mask_BxS2_bk0': mask_BxS2_bk0, 'L0_xattn_Wq': _L0_xattn_in['Wq'], 'L0_xattn_bq': _L0_xattn_in['bq'], 'L0_xattn_Wk': _L0_xattn_in['Wk'], 'L0_xattn_bk': _L0_xattn_in['bk'], 'L0_xattn_Wv': _L0_xattn_in['Wv'], 'L0_xattn_bv': _L0_xattn_in['bv'], 'L0_xattn_Wo': _L0_xattn_in['Wo'], 'L0_xattn_bo': _L0_xattn_in['bo'], 'L0_attn_Wq': _L0_attn_in['Wq'], 'L0_attn_Wk': _L0_attn_in['Wk'], 'L0_attn_Wv': _L0_attn_in['Wv'], 'L0_attn_Wo': _L0_attn_in['Wo'], 'L0_attn_lambda_q1': _L0_attn_in['lambda_q1'], 'L0_attn_lambda_k1': _L0_attn_in['lambda_k1'], 'L0_attn_lambda_q2': _L0_attn_in['lambda_q2'], 'L0_attn_lambda_k2': _L0_attn_in['lambda_k2'], 'L0_attn_rms_scale': _L0_attn_in['rms_scale'], 'L0_ffn_gate_w': _L0_ffn_in['gate_w'], 'L0_ffn_gate_b': _L0_ffn_in['gate_b'], 'L0_ffn_w1': _L0_ffn_in['w1'], 'L0_ffn_b1': _L0_ffn_in['b1'], 'L0_ffn_w3': _L0_ffn_in['w3'], 'L0_ffn_b3': _L0_ffn_in['b3'], 'L0_ffn_w2': _L0_ffn_in['w2'], 'L0_ffn_b2': _L0_ffn_in['b2'], 'L0_ffn_sw1': _L0_ffn_in['sw1'], 'L0_ffn_sb1': _L0_ffn_in['sb1'], 'L0_ffn_sw3': _L0_ffn_in['sw3'], 'L0_ffn_sb3': _L0_ffn_in['sb3'], 'L0_ffn_sw2': _L0_ffn_in['sw2'], 'L0_ffn_sb2': _L0_ffn_in['sb2'], 'L1_xattn_Wq': _L1_xattn_in['Wq'], 'L1_xattn_Wkv': _L1_xattn_in['Wkv'], 'L1_xattn_Wout': _L1_xattn_in['Wout'], 'L1_xattn_bout': _L1_xattn_in['bout'], 'L1_xattn_g_media': _L1_xattn_in['g_media'], 'L1_xattn_b_media': _L1_xattn_in['b_media'], 'L1_xattn_g_latent': _L1_xattn_in['g_latent'], 'L1_xattn_b_latent': _L1_xattn_in['b_latent'], 'L1_attn_Wq': _L1_attn_in['Wq'], 'L1_attn_Wk': _L1_attn_in['Wk'], 'L1_attn_Wo': _L1_attn_in['Wo'], 'L1_attn_U_b': _L1_attn_in['U_b'], 'L1_attn_V_b': _L1_attn_in['V_b'], 'L1_attn_W_b': _L1_attn_in['W_b'], 'L1_attn_bias_b': _L1_attn_in['bias_b'], 'L1_attn_U_t': _L1_attn_in['U_t'], 'L1_attn_V_t': _L1_attn_in['V_t'], 'L1_attn_W_t': _L1_attn_in['W_t'], 'L1_attn_X_t': _L1_attn_in['X_t'], 'L1_attn_bias_t': _L1_attn_in['bias_t'], 'L1_attn_alpha': _L1_attn_in['alpha'], 'L1_ffn_gate_w': _L1_ffn_in['gate_w'], 'L1_ffn_w1': _L1_ffn_in['w1'], 'L1_ffn_b1': _L1_ffn_in['b1'], 'L1_ffn_w2': _L1_ffn_in['w2'], 'L1_ffn_b2': _L1_ffn_in['b2']}

def reference(x, ctx_1024, mask_BxS2_bk0, L0_xattn_Wq, L0_xattn_bq, L0_xattn_Wk, L0_xattn_bk, L0_xattn_Wv, L0_xattn_bv, L0_xattn_Wo, L0_xattn_bo, L0_attn_Wq, L0_attn_Wk, L0_attn_Wv, L0_attn_Wo, L0_attn_lambda_q1, L0_attn_lambda_k1, L0_attn_lambda_q2, L0_attn_lambda_k2, L0_attn_rms_scale, L0_ffn_gate_w, L0_ffn_gate_b, L0_ffn_w1, L0_ffn_b1, L0_ffn_w3, L0_ffn_b3, L0_ffn_w2, L0_ffn_b2, L0_ffn_sw1, L0_ffn_sb1, L0_ffn_sw3, L0_ffn_sb3, L0_ffn_sw2, L0_ffn_sb2, L1_xattn_Wq, L1_xattn_Wkv, L1_xattn_Wout, L1_xattn_bout, L1_xattn_g_media, L1_xattn_b_media, L1_xattn_g_latent, L1_xattn_b_latent, L1_attn_Wq, L1_attn_Wk, L1_attn_Wo, L1_attn_U_b, L1_attn_V_b, L1_attn_W_b, L1_attn_bias_b, L1_attn_U_t, L1_attn_V_t, L1_attn_W_t, L1_attn_X_t, L1_attn_bias_t, L1_attn_alpha, L1_ffn_gate_w, L1_ffn_w1, L1_ffn_b1, L1_ffn_w2, L1_ffn_b2):
    import jax
    import jax.numpy as jnp

    def _L0_xattn_ref(query, key, value, Wq, bq, Wk, bk, Wv, bv, Wo, bo):
        import jax, jax.numpy as jnp
        import numpy as np
        H = 16
        D_MODEL = 128
        D_K = D_MODEL // H

        def _split_heads(x, B, T):
            return x.reshape(B, T, H, D_K).transpose(0, 2, 1, 3)
        B, T, _ = query.shape
        q = _split_heads(query @ Wq.T + bq, B, T)
        k = _split_heads(key @ Wk.T + bk, B, key.shape[1])
        v = _split_heads(value @ Wv.T + bv, B, value.shape[1])
        scores = jnp.einsum('bhqd,bhkd->bhqk', q, k) / jnp.sqrt(jnp.float32(D_K)).astype(q.dtype)
        weights = jax.nn.softmax(scores, axis=-1)
        x = jnp.einsum('bhqk,bhkd->bhqd', weights, v)
        x = x.transpose(0, 2, 1, 3).reshape(B, T, H * D_K)
        return x @ Wo.T + bo

    def _L0_attn_ref(X, Wq, Wk, Wv, Wo, lambda_q1, lambda_k1, lambda_q2, lambda_k2, rms_scale):
        import jax, jax.numpy as jnp
        import numpy as np
        D_MODEL = 128
        NUM_HEADS = 16
        D_HEAD = D_MODEL // NUM_HEADS
        LAMBDA_INIT = 0.8
        EPS = 1e-05
        B, N, _ = X.shape
        H, Dh = (NUM_HEADS, D_HEAD)
        Q = (X @ Wq).reshape(B, N, H, 2 * Dh).transpose(0, 2, 1, 3)
        K = (X @ Wk).reshape(B, N, H, 2 * Dh).transpose(0, 2, 1, 3)
        V = (X @ Wv).reshape(B, N, H, 2 * Dh).transpose(0, 2, 1, 3)
        Q1, Q2 = (Q[..., :Dh], Q[..., Dh:])
        K1, K2 = (K[..., :Dh], K[..., Dh:])
        lam = jnp.exp(jnp.sum(lambda_q1 * lambda_k1, -1)) - jnp.exp(jnp.sum(lambda_q2 * lambda_k2, -1)) + LAMBDA_INIT
        scaling = 1.0 / np.sqrt(Dh)
        causal = jnp.tril(jnp.ones((N, N), bool))
        neg_inf = jnp.float32(-jnp.inf)
        A1 = jnp.einsum('bhqd,bhkd->bhqk', Q1, K1) * scaling
        A2 = jnp.einsum('bhqd,bhkd->bhqk', Q2, K2) * scaling
        A1 = jnp.where(causal, A1, neg_inf)
        A2 = jnp.where(causal, A2, neg_inf)
        attn = jax.nn.softmax(A1, axis=-1) - lam[None, :, None, None] * jax.nn.softmax(A2, axis=-1)
        O = jnp.einsum('bhqk,bhkd->bhqd', attn, V)
        rms = jnp.sqrt(jnp.mean(O * O, axis=-1, keepdims=True) + EPS)
        O = O / rms * rms_scale
        O = O * (1.0 - LAMBDA_INIT)
        O = O.transpose(0, 2, 1, 3).reshape(B, N, H * 2 * Dh)
        return O @ Wo

    def _L0_ffn_ref(x, gate_w, gate_b, w1, b1, w3, b3, w2, b2, sw1, sb1, sw3, sb3, sw2, sb2):
        import jax, jax.numpy as jnp
        import numpy as np
        E = 8
        TOP_K = 2
        ROUTE_SCALE = 1.0
        ALPHA = 1.702
        LIMIT = 7.0
        D = 128
        F = 128
        B, S = (2, 128)

        def swiglu(h):
            g = jnp.minimum(h[..., ::2], LIMIT)
            l = jnp.clip(h[..., 1::2], -LIMIT, LIMIT)
            return g * jax.nn.sigmoid(ALPHA * g) * (l + 1.0)
        if __name__ == '__main__':
            out = reference(**setup_inputs())
            print(out.shape, out.dtype)
        inp_shape = x.shape
        xt = x.reshape(-1, D)
        logits = xt @ gate_w.T
        scores = jax.nn.softmax(logits.astype(jnp.float32), axis=-1)
        biased = scores + gate_b.astype(jnp.float32)
        idx = jax.lax.top_k(biased, TOP_K)[1]
        weights = (jnp.take_along_axis(scores, idx, axis=-1) * ROUTE_SCALE).astype(x.dtype)
        cw = jnp.sum(jax.nn.one_hot(idx, E, dtype=x.dtype) * weights[..., None], axis=1)
        h1 = jnp.einsum('td,efd->etf', xt, w1) + b1[:, None, :]
        h3 = jnp.einsum('td,efd->etf', xt, w3) + b3[:, None, :]
        a = swiglu(h1 * h3)
        y = jnp.einsum('etf,edf->etd', a, w2) + b2[:, None, :]
        routed = jnp.einsum('te,etd->td', cw, y)
        sh = swiglu((xt @ sw1.T + sb1) * (xt @ sw3.T + sb3))
        shared = sh @ sw2.T + sb2
        return (routed + shared).reshape(inp_shape)

    def _L1_xattn_ref(x, latents, mask, Wq, Wkv, Wout, bout, g_media, b_media, g_latent, b_latent):
        import jax, jax.numpy as jnp
        import numpy as np
        DIM = 128
        DIM_HEAD = 64
        NUM_HEADS = 16
        HIDDEN = DIM_HEAD * NUM_HEADS
        EPS = 1e-05

        def layer_norm(t, gamma, beta):
            mu = jnp.mean(t, axis=-1, keepdims=True)
            var = jnp.var(t, axis=-1, keepdims=True)
            return (t - mu) * jax.lax.rsqrt(var + EPS) * gamma + beta
        B, F, _ = x.shape
        Q = latents.shape[1]
        scale = DIM_HEAD ** (-0.5)
        xn = layer_norm(x, g_media, b_media)
        ln = layer_norm(latents, g_latent, b_latent)
        q = (ln @ Wq).reshape(B, Q, NUM_HEADS, DIM_HEAD).transpose(0, 2, 1, 3) * scale
        kv_input = jnp.concatenate([xn, ln], axis=1)
        kv = kv_input @ Wkv
        k, v = jnp.split(kv, 2, axis=-1)
        k = k.reshape(B, F + Q, NUM_HEADS, DIM_HEAD).transpose(0, 2, 1, 3)
        v = v.reshape(B, F + Q, NUM_HEADS, DIM_HEAD).transpose(0, 2, 1, 3)
        sim = jnp.einsum('bhqd,bhfd->bhqf', q, k)
        latent_mask = jnp.zeros((B, Q), dtype=bool)
        full_mask = jnp.concatenate([mask, latent_mask], axis=1)
        max_neg = -jnp.finfo(sim.dtype).max
        sim = jnp.where(full_mask[:, None, None, :], max_neg, sim)
        alphas = jax.nn.softmax(sim, axis=-1)
        out = jnp.einsum('bhqf,bhfv->bhqv', alphas, v)
        out = out.transpose(0, 2, 1, 3).reshape(B, Q, HIDDEN)
        return out @ Wout + bout

    def _L1_attn_ref(x, Wq, Wk, Wo, U_b, V_b, W_b, bias_b, U_t, V_t, W_t, X_t, bias_t, alpha):
        import jax, jax.numpy as jnp
        import numpy as np
        D_MODEL = 128
        RANK = 32
        INIT_ALPHA = 0.5
        B, T, D = x.shape
        Q = x @ Wq.T
        K = x @ Wk.T
        counts = jnp.arange(1, T + 1, dtype=x.dtype)[None, :, None]
        Z = jnp.cumsum(x, axis=1) / counts
        a_b = Q @ V_b
        c_b = jnp.cumsum(K @ W_b, axis=1)
        bil = a_b * c_b @ U_b.T
        a_t = Q @ V_t
        c_t = jnp.cumsum(K @ W_t, axis=1)
        z_t = Z @ X_t
        tri = a_t * z_t * c_t @ U_t.T
        out = (bil + alpha * tri) / counts + (bias_b + alpha * bias_t)
        return out @ Wo.T

    def _L1_ffn_ref(x, gate_w, w1, b1, w2, b2):
        import jax, jax.numpy as jnp
        import numpy as np
        D_MODEL = 128
        NUM_EXPERTS = 8
        HIDDEN = 512
        TOP_K = 2
        B, S, D = x.shape
        xf = x.reshape(-1, D)
        T = xf.shape[0]
        gate_logits = xf @ gate_w.T
        gate_probs = jax.nn.softmax(gate_logits, axis=-1)
        topk_scores, topk_idx = jax.lax.top_k(gate_probs, TOP_K)
        topk_scores = topk_scores / jnp.sum(topk_scores, axis=-1, keepdims=True)
        combine = jnp.zeros((T, NUM_EXPERTS), dtype=x.dtype)
        combine = combine.at[jnp.arange(T)[:, None], topk_idx].set(topk_scores)
        h = jax.nn.relu(jnp.einsum('td,ehd->teh', xf, w1) + b1)
        expert_out = jnp.einsum('teh,edh->ted', h, w2) + b2
        out = jnp.einsum('ted,te->td', expert_out, combine)
        return out.reshape(B, S, D)
    x = x + _L0_xattn_ref(_layernorm(x, axis=-1), ctx_1024, ctx_1024, L0_xattn_Wq, L0_xattn_bq, L0_xattn_Wk, L0_xattn_bk, L0_xattn_Wv, L0_xattn_bv, L0_xattn_Wo, L0_xattn_bo)
    x = x + _L0_attn_ref(_layernorm(x, axis=-1), L0_attn_Wq, L0_attn_Wk, L0_attn_Wv, L0_attn_Wo, L0_attn_lambda_q1, L0_attn_lambda_k1, L0_attn_lambda_q2, L0_attn_lambda_k2, L0_attn_rms_scale)
    x = x + _L0_ffn_ref(_layernorm(x, axis=-1), L0_ffn_gate_w, L0_ffn_gate_b, L0_ffn_w1, L0_ffn_b1, L0_ffn_w3, L0_ffn_b3, L0_ffn_w2, L0_ffn_b2, L0_ffn_sw1, L0_ffn_sb1, L0_ffn_sw3, L0_ffn_sb3, L0_ffn_sw2, L0_ffn_sb2)
    x = x + _L1_xattn_ref(ctx_1024, _layernorm(x, axis=-1), mask_BxS2_bk0, L1_xattn_Wq, L1_xattn_Wkv, L1_xattn_Wout, L1_xattn_bout, L1_xattn_g_media, L1_xattn_b_media, L1_xattn_g_latent, L1_xattn_b_latent)
    x = x + _L1_attn_ref(_layernorm(x, axis=-1), L1_attn_Wq, L1_attn_Wk, L1_attn_Wo, L1_attn_U_b, L1_attn_V_b, L1_attn_W_b, L1_attn_bias_b, L1_attn_U_t, L1_attn_V_t, L1_attn_W_t, L1_attn_X_t, L1_attn_bias_t, L1_attn_alpha)
    x = x + _L1_ffn_ref(_layernorm(x, axis=-1), L1_ffn_gate_w, L1_ffn_w1, L1_ffn_b1, L1_ffn_w2, L1_ffn_b2)
    return x

_drawn_inputs = setup_inputs


def setup_inputs(seed=0):
    import zlib

    import numpy as np

    out = dict(_drawn_inputs(seed))
    spreads = {'L0_xattn_bq': (0.0, 0.1),
     'L0_xattn_bk': (0.0, 2.0),
     'L0_xattn_bv': (0.0, 0.1),
     'L0_xattn_bo': (0.0, 0.1),
     'L0_attn_rms_scale': (1.0, 0.2),
     'L1_xattn_bout': (0.0, 0.1),
     'L1_xattn_g_media': (1.0, 0.2),
     'L1_xattn_b_media': (0.0, 0.1),
     'L1_xattn_g_latent': (1.0, 0.2),
     'L1_xattn_b_latent': (0.0, 0.271),
     'L1_attn_bias_b': (0.0, 0.428),
     'L1_attn_bias_t': (0.0, 0.445)}
    factors = {'L0_ffn_b1': 5.695,
     'L0_ffn_b3': 12.392,
     'L0_ffn_b2': 13.437,
     'L0_ffn_sb1': 3.494,
     'L0_ffn_sb2': 3.055,
     'L1_attn_Wq': 8.0,
     'L1_attn_Wk': 8.0,
     'L1_attn_Wo': 3.006,
     'L1_attn_U_b': 8.0,
     'L1_attn_V_b': 8.0,
     'L1_attn_W_b': 8.0,
     'L1_attn_U_t': 8.0,
     'L1_attn_V_t': 8.0,
     'L1_attn_W_t': 8.0,
     'L1_attn_X_t': 8.0,
     'L1_ffn_b1': 52.573,
     'L1_ffn_b2': 35.9,
     'L0_ffn_sb3': 5.817}
    for name, (base, spread) in spreads.items():
        noise = np.random.default_rng([zlib.crc32(name.encode()), seed]).standard_normal(out[name].shape)
        drawn = base * np.exp(spread * noise) if base else spread * noise
        out[name] = jnp.asarray(drawn.astype(out[name].dtype))
    for name, factor in factors.items():
        out[name] = (out[name] * factor).astype(out[name].dtype)
    return out
```

```python
from contextlib import ExitStack

import numpy as np
import concourse.bass as bass
from concourse import mybir

F32 = mybir.dt.float32
BF16 = mybir.dt.bfloat16
U8 = mybir.dt.uint8
U32 = mybir.dt.uint32
ALU = mybir.AluOpType
ACT = mybir.ActivationFunctionType
AX = mybir.AxisListType.X

P = 128
D = 128
B = 8
Q = 32
T = B * Q
NT = T // P
BT = B // NT
S = 512
C = S // P
G = 4
HG = 4
HALF_H = 64
HH = 2
E = 8
RAW_SLOTS = 4
NE0 = E + 1
KH = 4
SL = S + Q
NEG = -float(2.0 ** 127)
LN_EPS = 1e-5
RING = 3
ROWS = 54


def broadcast(ap, axis, n):
    ap = ap.unsqueeze(axis)
    shape = list(ap.shape)
    shape[axis] = n
    return ap.to_broadcast(shape)


def ring_jobs():
    jobs = ["w0T", "rowsT", "bias0T", ("xT", 0), "q0T"]
    for b in range(2):
        jobs += [("ctxT", b), ("k0T", b), ("v0", b)]
    for i in range(B + 1):
        jobs += [("fill", i, n) for n in range(len(FILL[i]))]
        if i + 2 < B:
            jobs += [("ctxT", i + 2), ("k0T", i + 2), ("v0", i + 2)]
        if i >= 1:
            jobs += [("p0T", i - 1, c) for c in range(C)]
    jobs += ["o0", ("xT", 1), "qd", "kd"] + [("vd", i) for i in range(4)]
    jobs += [("odT", t) for t in range(NT)] + ["od"]
    jobs += [("xT", 2), "gate0", "cw0T"] + [("y0", i) for i in range(NE0)]
    jobs += [("xT", 3)] + [("q1T", i) for i in range(4)] + [("qk", i) for i in range(8)]
    for i in range(B + 1):
        jobs += [("fill1", i, n) for n in range(len(FILL1[i]))]
        if i >= 1:
            jobs += [("p1T", i - 1, c) for c in range(C + 1)]
    jobs += [("o1T", i) for i in range(4)] + ["o1", ("xT", 4), "ac", "z", "ol"]
    jobs += [("xT", 5), "gate1", "cw1T"] + [("y1", i) for i in range(E)] + ["b1y"]
    return jobs


FILL = [[("w2T", 0), ("w2T", 1)], [("w2T", 2), ("m12",)], [("woT",), ("g",), ("w13T", 0), ("w13T", 1)],
        [("w13T", 2), ("w13T", 3), ("xnT", 0)], [("w13T", 8), ("w13T", 4), ("xnT", 1)],
        [("w13T", 5), ("w13T", 6), ("w13T", 7), ("xnT", 2)],
        [("wkT", 0), ("wkT", 1), ("xnT", 3), ("xnT", 4)], [("xnT", 5), ("w11T", 0)],
        [("xnT", 6), ("xnT", 7), ("w11T", 1), ("w11T", 2), ("w11T", 3)]]
FILL1 = [[("w11T", 4), ("w11T", 5)], [("w11T", 6), ("w11T", 7)], [("w12T", 0)], [("w12T", 1)], [("w12T", 2)],
         [("w12T", 3)], [("w12T", 4), ("w12T", 5)], [("w12T", 6), ("w12T", 7)], []]
ON_ACT = {"w11T", "xnT", "w12T"}


def build(nc, d, out):
    with ExitStack() as ctx:
        def sb(name, shape, dt=F32):
            return ctx.enter_context(nc.sbuf_tensor(name, shape, dt))

        def sem(name):
            return ctx.enter_context(nc.semaphore(name))

        job = {key: i for i, key in enumerate(ring_jobs())}
        weight_job = {what: ("fill", i, n) for i, fs in enumerate(FILL) for n, what in enumerate(fs)}
        weight_job |= {what: ("fill1", i, n) for i, fs in enumerate(FILL1) for n, what in enumerate(fs)}

        banks = ctx.enter_context(nc.psum_tensor("banks", [P, 8, 512], F32))
        acc = banks[:, 4, :]

        x_sb = sb("x_sb", [P, NT, D])
        xb_sb = sb("xb_sb", [P, NT, D])
        xln = sb("xln", [P, NT, D])
        lat = sb("lat", [P, NT, D])
        xT = sb("xT", [P, T])
        ctx_sb = sb("ctx_sb", [P, B, C, D])
        ctxT = sb("ctxT", [P, B, C, P])
        k0T = sb("k0T", [P, B, S])
        v0 = sb("v0", [P, B, C, D])
        xnT = sb("xnT", [P, B, S])
        w11T = sb("w11T", [P, E, KH, P])
        w13T = sb("w13T", [P, NE0, 4, P])
        w2T = sb("w2T", [P, NE0, D])
        w0T = sb("w0T", [P, 4, D])
        cols = sb("cols", [P, ROWS])
        bcol = sb("bcol", [P, 2, 2 * NE0])
        bc = sb("bc", [P, 6, D])
        gb = sb("gb", [P, E])
        alpha = sb("alpha", [P, 1])
        self_w = sb("self_w", [P, 8 * D])
        ws = self_w[:, 0:6 * D].rearrange("p (i n) -> p i n", i=3)
        wso = self_w[:, 6 * D:].rearrange("p (i n) -> p i n", i=2)
        wkv1 = sb("wkv1", [P, 32 * HALF_H])
        wout1 = sb("wout1", [P, 8, D])
        wkT = sb("wkT", [P, 8, D])
        lowr = sb("lowr", [P, 5, 32])
        uu = sb("uu", [P, 65])
        m12 = sb("m12", [P, P])
        woT = sb("woT", [P, D])
        gl = sb("gl", [65, D])
        b2x = sb("b2x", [NE0, D])
        b2y = sb("b2y", [E, D])
        negmask = sb("negmask", [P, B, SL], BF16)

        ident = sb("ident", [P, P])
        sel16 = sb("sel16", [P, 16])
        sel4 = sb("sel4", [P, 4])
        mask4 = sb("mask4", [P, 4])
        mask4s = sb("mask4s", [P, 4])
        mask2 = sb("mask2", [P, 2])
        caus3 = sb("caus3", [P, 4, Q])
        causal = sb("causal", [P, Q])
        half_a = sb("half_a", [P, 1])
        half_b = sb("half_b", [P, 1])
        lam_c = sb("lam_c", [P, 8])
        iota8 = sb("iota8", [P, E])
        minus_half = sb("minus_half", [P, 16])
        icnt = sb("icnt", [64, B, Q])
        keep = sb("keep", [64, B, Q])

        qT = sb("qT", [P, T])
        big = sb("big", [P, 8, SL])
        pT = sb("pT", [P, C + 1, 512])
        stats = sb("stats", [P, 40, 6])
        mv = sb("mv", [P, 40, 2])
        rstd = sb("rstd", [P, 40])
        nmr = sb("nmr", [P, 40])
        nmax = sb("nmax", [P, 2 * B * G])
        rsum = sb("rsum", [P, 2 * B * G])
        rinv = sb("rinv", [P, 2 * B * G])
        oT = sb("oT", [P, 8, T])
        small = sb("small", [P, 16, 2, 16])
        m8 = sb("m8", [P, 2, 8])
        ix = sb("ix", [P, 2, 8], U32)
        cw = sb("cw", [P, 2, NE0])
        cwT = sb("cwT", [NE0, T])

        def flat(t):
            names = "abcde"[:len(t.shape) - 1]
            return t[:].rearrange(f"p {' '.join(names)} -> p ({' '.join(names)})") if len(names) > 1 else t[:]

        def view(t, first, *shape, parts=P):
            v = flat(t)[0:parts, first:first + int(np.prod(shape))]
            names = "abcde"[:len(shape)]
            sizes = dict(zip(names, shape))
            return v.rearrange(f"p ({' '.join(names)}) -> p {' '.join(names)}", **sizes) if len(names) > 1 else v

        w0raw = view(k0T, 6 * S, 4, D)
        shared_raw = view(k0T, 7 * S, 4, D)
        wl = view(k0T, 4 * S, 3, D)
        rows = view(k0T, 5 * S, D, parts=ROWS)
        brow = view(k0T, 5 * S + D, 2 * P, parts=2 * NE0)
        w2raw = view(v0, 5 * S, NE0, P)
        w1raw0 = view(w11T, 0, 2, 2 * E, D)
        lam_in = view(lat, 0, 4, 8, 8)
        wraw1 = view(ctxT, 0, RAW_SLOTS, KH, D)
        qblk_d = view(ctxT, RAW_SLOTS * KH * D, 2 * B, HG, Q)
        qblk_c = view(oT, 4 * T, B, HG, Q)
        kdT = view(oT, 2 * T, 2, T)
        own = view(oT, 2 * T, 2 * T)
        vblk = view(big, 4 * SL, B * 8, 2, 16)
        mask_u8 = k0T[:].bitcast(U8).rearrange("p b s -> p (b s)")[:, 0:B * S].rearrange("p (b s) -> p b s", b=B)
        qk = view(k0T, 0, B, 16, Q)
        yT = view(v0, 0, 16, T)
        wq1 = view(self_w, 0, 16 * HALF_H)
        w12T = view(w13T, 0, E, KH, P)
        hid = view(big, 0, 2, KH, T)
        tmp = view(pT, 0, 6, T)
        x_rep = view(pT, 0, B, 4, Q)
        scan = view(big, 0, 4, T, parts=65)

        x_loaded = sem("x_loaded")
        w0_loaded = sem("w0_loaded")
        rows_loaded = sem("rows_loaded")
        ctx_loaded = [sem(f"ctx_loaded{b}") for b in range(B)]
        bc_loaded = sem("bc_loaded")
        mask_loaded = sem("mask_loaded")
        self_loaded = sem("self_loaded")
        exp0_loaded = [sem(f"exp0_loaded{h}") for h in range(2)]
        exp0_w2_loaded = sem("exp0_w2_loaded")
        b2_loaded = sem("b2_loaded")
        lat_loaded = sem("lat_loaded")
        wq1_loaded = sem("wq1_loaded")
        lin_loaded = sem("lin_loaded")
        exp1_loaded = [sem(f"exp1_loaded{s}") for s in range(RAW_SLOTS)]
        out_stored = sem("out_stored")
        pool_step = sem("pool_step")
        dve_step = sem("dve_step")
        act_step = sem("act_step")
        ring_filled = [sem(f"ring_filled{i}") for i in range(RING)]
        ring_copied = [sem(f"ring_copied{i}") for i in range(RING)]
        ident_ready = sem("ident_ready")
        consts_ready = sem("consts_ready")
        consts2_ready = sem("consts2_ready")
        negmask_ready = sem("negmask_ready")
        bias_added = sem("bias_added")
        ln_var = sem("ln_var")
        ln_rstd = sem("ln_rstd")
        ln_done = sem("ln_done")
        cstat_ready = sem("cstat_ready")
        xn_ready = sem("xn_ready")
        qblk_ready = sem("qblk_ready")
        s_filled = sem("s_filled")
        s_max = sem("s_max")
        s_exp = sem("s_exp")
        s_rinv = sem("s_rinv")
        p_ready = sem("p_ready")
        av_read = sem("av_read")
        acc_filled = sem("acc_filled")
        acc_read = sem("acc_read")
        o0T_ready = sem("o0T_ready")
        x_final = sem("x_final")
        d_filled = sem("d_filled")
        d_max = sem("d_max")
        d_sub = sem("d_sub")
        d_exp = sem("d_exp")
        d_sum = sem("d_sum")
        d_norm = sem("d_norm")
        d_pT = sem("d_pT")
        d_sq = sem("d_sq")
        d_ms = sem("d_ms")
        d_rms = sem("d_rms")
        d_on = sem("d_on")
        vblk_ready = sem("vblk_ready")
        wso_ready = sem("wso_ready")
        lam_sum = sem("lam_sum")
        lam_exp = sem("lam_exp")
        uu_ready = sem("uu_ready")
        g_max = sem("g_max")
        g_exp = sem("g_exp")
        cw_ready = sem("cw_ready")
        h_filled = sem("h_filled")
        h_act = sem("h_act")
        h_dve = sem("h_dve")
        gate_ready = sem("gate_ready")
        tanh_ready = sem("tanh_ready")
        lin_ready = sem("lin_ready")
        a_ready = sem("a_ready")
        pr_ready = sem("pr_ready")

        block = ctx.enter_context(nc.Block())

        def slot_use(key):
            i = job[weight_job.get(key, key)]
            return i % RING, i // RING

        def bank(key):
            return banks[:, 5 + slot_use(key)[0], :]

        def wait_bank_free(pe, key):
            s, n = slot_use(key)
            if n:
                pe.wait_ge(ring_copied[s], n)

        def wait_filled(eng, key):
            s, n = slot_use(key)
            eng.wait_ge(ring_filled[s], n + 1)

        def wait_copied(eng, key):
            s, n = slot_use(key)
            eng.wait_ge(ring_copied[s], n + 1)

        def filled(ins, key):
            ins.then_inc(ring_filled[slot_use(key)[0]], 1)

        def copied(ins, key):
            ins.then_inc(ring_copied[slot_use(key)[0]], 1)

        @block.sync
        def _(sp):
            def load(dst, src, loaded):
                sp.dma_start(dst, src).then_inc(loaded, 16)

            load(x_sb[:], d["x"].rearrange("b q d -> (b q) d").rearrange("(t p) d -> p t d", p=P), x_loaded)
            for i, n in enumerate(("Wq", "Wk", "Wv", "Wo")):
                load(w0raw[:, i, :], d["L0_xattn_" + n], w0_loaded)
            for i, n in enumerate(("L0_xattn_bq", "L0_xattn_bk", "L0_xattn_bv", "L1_attn_bias_b", "L1_attn_bias_t")):
                load(rows[i:i + 1, :], d[n].rearrange("(o n) -> o n", o=1), rows_loaded)
            load(rows[5:6, :].rearrange("o (h d) -> o h d", d=16),
                 broadcast(d["L0_attn_rms_scale"].rearrange("(o n) -> o n", o=1), 1, 8), rows_loaded)
            load(rows[6:14, :], d["L0_ffn_gate_w"], rows_loaded)
            load(rows[14:22, :], d["L1_ffn_gate_w"], rows_loaded)
            load(rows[22:54, :], d["L1_ffn_b1"].rearrange("e (k p) -> (e k) p", p=P), rows_loaded)
            load(brow[0:E, :], d["L0_ffn_b1"], rows_loaded)
            load(brow[E:E + 1, :], d["L0_ffn_sb1"].rearrange("(o n) -> o n", o=1), rows_loaded)
            load(brow[NE0:NE0 + E, :], d["L0_ffn_b3"], rows_loaded)
            load(brow[NE0 + E:, :], d["L0_ffn_sb3"].rearrange("(o n) -> o n", o=1), rows_loaded)

            def load_ctx(b):
                load(ctx_sb[:, b, :, :], d["ctx_1024"][b].rearrange("(p c) d -> p c d", c=C), ctx_loaded[b])

            for b in range(3):
                load_ctx(b)
            for i, n in enumerate(("L0_xattn_bo", "L1_xattn_bout", "L1_xattn_g_media", "L1_xattn_b_media",
                                   "L1_xattn_g_latent", "L1_xattn_b_latent")):
                load(bc[:, i, :], d[n].partition_broadcast(P), bc_loaded)
            load(gb[:], d["L0_ffn_gate_b"].partition_broadcast(P), bc_loaded)
            load(alpha[:], d["L1_attn_alpha"].partition_broadcast(P), bc_loaded)
            load(w2raw[:, 0:E, :], d["L0_ffn_w2"].rearrange("e d f -> d e f"), exp0_w2_loaded)
            load(w2raw[:, E, :], d["L0_ffn_sw2"], exp0_w2_loaded)
            for i, n in enumerate(("Wq", "Wk", "Wo")):
                load(wl[:, i, :], d["L1_attn_" + n], lin_loaded)
            for i, n in enumerate(("V_b", "V_t", "W_b", "W_t", "X_t")):
                load(lowr[:, i, :], d["L1_attn_" + n], lin_loaded)
            load(uu[:, 0:32], d["L1_attn_U_b"], lin_loaded)
            load(uu[:, 32:64], d["L1_attn_U_t"], lin_loaded)
            load_ctx(3)
            load_ctx(4)
            w1v = "e (i r) d -> i e r d"
            for h in range(2):
                es = slice(4 * h, 4 * h + 4)
                for w, n in enumerate(("L0_ffn_w1", "L0_ffn_w3")):
                    load(w1raw0[:, w, 8 * h:8 * h + 8, :].rearrange("p (e r) d -> p e r d", r=2),
                         d[n][es].rearrange(w1v, r=2), exp0_loaded[h])
                if h == 0:
                    load_ctx(5)
            for w, n in enumerate(("L0_ffn_sw1", "L0_ffn_sw3")):
                load(shared_raw[:, 2 * w:2 * w + 2, :], d[n].rearrange("(i r) d -> i r d", r=2), exp0_loaded[1])
            load_ctx(6)
            load_ctx(7)
            load(b2x[0:E, :], d["L0_ffn_b2"], b2_loaded)
            load(b2x[E:, :], d["L0_ffn_sb2"].rearrange("(o n) -> o n", o=1), b2_loaded)
            load(b2y[:], d["L1_ffn_b2"], b2_loaded)
            for i, n in enumerate(("Wq", "Wk", "Wv")):
                load(ws[:, i, :], d["L0_attn_" + n], self_loaded)
            load(wso, d["L0_attn_Wo"].rearrange("(t p) d -> p t d", p=P), self_loaded)
            for i, n in enumerate(("q1", "k1", "q2", "k2")):
                v = d["L0_attn_lambda_" + n].rearrange("(g h) d -> h g d", h=2)
                for h in range(2):
                    load(lam_in[64 * h:64 * h + 64, i, :, :], v[h].partition_broadcast(64), self_loaded)
            load(wkv1[:], d["L1_xattn_Wkv"], lat_loaded)
            load(wout1[:], d["L1_xattn_Wout"].rearrange("(i p) n -> p i n", p=P), lat_loaded)
            wait_filled(sp, ("v0", B - 1))
            for e in range(RAW_SLOTS):
                load(wraw1[:, e], d["L1_ffn_w1"][e].rearrange("(k p) d -> p k d", p=P), exp1_loaded[e])
            sp.wait_ge(s_filled, B * G)
            load(mask_u8, d["mask_BxS2_bk0"].partition_broadcast(P), mask_loaded)
            for e in range(RAW_SLOTS, E):
                wait_filled(sp, ("w11T", e - RAW_SLOTS))
                load(wraw1[:, e % RAW_SLOTS], d["L1_ffn_w1"][e].rearrange("(k p) d -> p k d", p=P), exp1_loaded[e % RAW_SLOTS])
            wait_filled(sp, "od")
            load(wq1, d["L1_xattn_Wq"], wq1_loaded)
            for e in range(E):
                wait_filled(sp, ("w11T", e + RAW_SLOTS) if e < RAW_SLOTS else ("w12T", e - RAW_SLOTS))
                load(wraw1[:, e % RAW_SLOTS].rearrange("p k d -> p (k d)"), d["L1_ffn_w2"][e], exp1_loaded[e % RAW_SLOTS])
            sp.wait_ge(x_final, 1)
            sp.dma_start(out.rearrange("b q d -> (b q) d").rearrange("(t p) d -> p t d", p=P), x_sb[:]).then_inc(out_stored, 16)
            sp.wait_ge(out_stored, 16)

        @block.gpsimd
        def _(pool):
            n = 0

            def step(ins):
                nonlocal n
                n += 1
                ins.then_inc(pool_step, 1)
                pool.wait_ge(pool_step, n)

            step(nc.gpsimd.memset(ident[:], 0.0))
            nc.gpsimd.affine_select(out=ident[:], in_=ident[:], compare_op=ALU.not_equal, fill=1.0, base=0,
                                    pattern=[[-1, P]], channel_multiplier=1).then_inc(ident_ready, 1)
            nc.gpsimd.memset(minus_half[:], -0.5)
            nc.gpsimd.memset(sel16[:], 1.0)
            nc.gpsimd.memset(sel4[:], 1.0)
            nc.gpsimd.memset(keep[:], 1.0)
            nc.gpsimd.memset(negmask[:, :, S:], 0.0)
            nc.gpsimd.memset(cw[:], 1.0)
            step(nc.gpsimd.memset(caus3[:], NEG))

            def select(ap, base, pattern):
                c, pattern = pattern[0], pattern[1:]
                step(nc.gpsimd.affine_select(out=ap, in_=ap, compare_op=ALU.is_ge, fill=0.0, base=base,
                                             pattern=pattern, channel_multiplier=c))

            select(sel16[:], 0, [1, [-8, 16]])
            select(sel16[:], 7, [-1, [8, 16]])
            select(sel4[:], 0, [1, [-Q, 4]])
            select(sel4[:], Q - 1, [-1, [Q, 4]])
            select(caus3[:], 0, [1, [-Q, 4], [0, Q]])
            select(caus3[:], Q - 1, [-1, [Q, 4], [0, Q]])
            select(caus3[:], -1, [-1, [Q, 4], [1, Q]])
            nc.gpsimd.iota(iota8[:], pattern=[[1, E]], base=0, channel_multiplier=0,
                           allow_small_or_imprecise_dtypes=True)
            step(nc.gpsimd.iota(icnt[:], pattern=[[0, B], [1, Q]], base=1, channel_multiplier=0,
                                allow_small_or_imprecise_dtypes=True))
            nc.gpsimd.memset(keep[:, :, 0:1], 0.0).then_inc(consts_ready, 1)

            def inv_sqrt(dst, src):
                return nc.gpsimd.tensor_tensor(dst, src, minus_half[:, 0:src.shape[1]], ALU.pow)

            def ln_of_x(k, cols_):
                pool.wait_ge(ln_var, k)
                inv_sqrt(rstd[:, cols_], rstd[:, cols_]).then_inc(ln_rstd, 1)

            ln_of_x(1, slice(32, 34))
            pool.wait_ge(bc_loaded, 16 * 8)
            pool.wait_ge(x_loaded, 16)
            nc.gpsimd.tensor_tensor(xb_sb[:], x_sb[:], broadcast(bc[:, 0, :], 1, NT), ALU.add).then_inc(bias_added, 1)

            def norm_ctx(b):
                cs = slice(C * b, C * b + C)
                pool.wait_ge(cstat_ready, b + 1)
                step(inv_sqrt(rstd[:, cs], rstd[:, cs]))
                step(nc.gpsimd.tensor_tensor(nmr[:, cs], nmr[:, cs], rstd[:, cs], ALU.mult))
                wait_filled(pool, ("ctxT", b))
                for c in range(C):
                    ins = nc.gpsimd.tensor_scalar(ctx_sb[:, b, c, :], ctx_sb[:, b, c, :], rstd[:, C * b + c:C * b + c + 1],
                                                  nmr[:, C * b + c:C * b + c + 1], ALU.mult, ALU.add)
                step(ins)
                step(nc.gpsimd.tensor_tensor(ctx_sb[:, b], ctx_sb[:, b], broadcast(bc[:, 2, :], 1, C), ALU.mult))
                nc.gpsimd.tensor_tensor(ctx_sb[:, b], ctx_sb[:, b], broadcast(bc[:, 3, :], 1, C), ALU.add).then_inc(xn_ready, 1)

            def normalise(b, first, width):
                pool.wait_ge(s_rinv, first // G + b + 1)
                for g in range(G):
                    i = first + G * b + g
                    t = big[:, (b % 2) * G + g, 0:width]
                    nc.gpsimd.tensor_scalar(t, t, rinv[:, i:i + 1], 1.0, ALU.mult, ALU.mult).then_inc(p_ready, 1)

            for b in range(B):
                norm_ctx(b)
                normalise(b, 0, S)
            pool.wait_ge(mask_loaded, 16)
            for b in range(B):
                ins = nc.gpsimd.tensor_scalar(negmask[:, b, 0:S].rearrange("q (c p) -> q c p", p=P),
                                              mask_u8[:, b, :].rearrange("q (p c) -> q c p", c=C), NEG, 1.0, ALU.mult, ALU.mult)
            ins.then_inc(negmask_ready, 1)
            ln_of_x(2, slice(34, 36))
            pool.wait_ge(d_ms, 1)
            inv_sqrt(small[:, 0, 0, :], small[:, 0, 0, :])
            inv_sqrt(small[:, 0, 1, :], small[:, 0, 1, :]).then_inc(d_rms, 1)
            ln_of_x(3, slice(36, 38))
            for i in range(NE0):
                pool.wait_ge(h_dve, i + 1)
                if i >= 2:
                    pool.wait_ge(a_ready, i - 1)
                nc.gpsimd.tensor_scalar(tmp[:, 4 + i % 2, :], tmp[:, 2 + i % 2, :], 7.0, -7.0, ALU.min, ALU.max).then_inc(lin_ready, 1)
            ln_of_x(4, slice(38, 40))
            ln_of_x(5, slice(38, 40))
            wait_copied(pool, ("y0", NE0 - 1))
            nc.gpsimd.tensor_tensor(xb_sb[:], x_sb[:], broadcast(bc[:, 1, :], 1, NT), ALU.add).then_inc(bias_added, 1)
            for b in range(B):
                normalise(b, B * G, SL)
            ln_of_x(6, slice(32, 34))
            ln_of_x(7, slice(34, 36))

        @block.scalar
        def _(act):
            n = 0

            def step(ins):
                nonlocal n
                n += 1
                ins.then_inc(act_step, 1)
                act.wait_ge(act_step, n)

            def copy_job(key, dst, src):
                wait_filled(act, key)
                copied(nc.scalar.activation(dst, src, ACT.Copy), key)

            copy_job("w0T", w0T[:].rearrange("p i d -> p (i d)"), bank("w0T"))
            copy_job("rowsT", cols[:], bank("rowsT")[:, 0:ROWS])
            copy_job("bias0T", bcol[:].rearrange("p r i -> p (r i)"), bank("bias0T")[:, 0:4 * NE0])
            copy_job(("xT", 0), xT[:], bank(("xT", 0))[:, 0:T])
            wait_filled(act, "q0T")
            wait_copied(act, "rowsT")
            copied(nc.scalar.activation(qT[:], bank("q0T")[:, 0:T], ACT.Identity, bias=cols[:, 0:1]), "q0T")

            def prep(b):
                copy_job(("ctxT", b), ctxT[:, b].rearrange("p c k -> p (c k)"), bank(("ctxT", b)))
                wait_filled(act, ("k0T", b))
                copied(nc.scalar.activation(k0T[:, b, :], bank(("k0T", b)), ACT.Identity, bias=cols[:, 1:2]), ("k0T", b))

            def weight(key):
                kind, e = key[0], key[-1]
                if kind == "xnT":
                    copy_job(key, xnT[:, e, :], bank(key))
                if kind == "w11T":
                    if e == 0:
                        wait_filled(act, ("w13T", E - 1))
                    copy_job(key, w11T[:, e].rearrange("p k m -> p (k m)"), bank(key))
                if kind == "w12T":
                    copy_job(key, w12T[:, e].rearrange("p k m -> p (k m)"), bank(key))

            for b in range(2):
                prep(b)
            for i in range(B + 1):
                if i < B:
                    for g in range(G):
                        k = G * i + g
                        act.wait_ge(s_max, k + 1)
                        if i >= 2:
                            wait_filled(act, ("p0T", i - 2, C - 1))
                        nc.scalar.activation(big[:, (i % 2) * G + g, 0:S], banks[:, g, :], ACT.Exp, bias=nmax[:, k:k + 1],
                                             accum_out=rsum[:, k:k + 1]).then_inc(s_exp, 1)
                for key in FILL[i]:
                    weight(key)
                if i + 2 < B:
                    prep(i + 2)
                if i >= 1:
                    for c in (0, 2):
                        if i >= 2:
                            act.wait_ge(av_read, C * (i - 2) + c + 1)
                        copy_job(("p0T", i - 1, c), pT[:, c, :], bank(("p0T", i - 1, c)))
            act.wait_ge(lam_sum, 1)
            nc.scalar.activation(small[:, 1:3, 0, 0:8], small[:, 1:3, 0, 0:8], ACT.Exp).then_inc(lam_exp, 1)
            wait_filled(act, ("xT", 1))
            step(nc.scalar.activation(xT[:], bank(("xT", 1))[:, 0:T], ACT.Copy))
            copied(nc.scalar.activation(x_rep, broadcast(bank(("xT", 1))[:, 0:T].rearrange("p (b q) -> p b q", q=Q), 2, 4), ACT.Copy),
                   ("xT", 1))
            copy_job("kd", kdT.rearrange("p r t -> p (r t)"), bank("kd"))
            for i in range(4):
                act.wait_ge(d_sub, i + 1)
                nc.scalar.activation(big[:, i, 0:S], big[:, i, 0:S], ACT.Exp).then_inc(d_exp, 1)
            act.wait_ge(acc_filled, 1)
            nc.scalar.activation(tmp[:, 0:2, :].rearrange("p t f -> p (t f)"), acc, ACT.Square).then_inc(d_sq, 1)
            for t in range(NT):
                copy_job(("odT", t), oT[:, 0:2, P * t:P * t + P], bank(("odT", t))[:, 0:2 * P].rearrange("p (f t) -> p f t", f=2))

            def gates(key, k):
                act.wait_ge(g_max, k)
                for t in range(NT):
                    ins = nc.scalar.activation(small[:, 3, t, 0:E], bank(key)[:, E * t:E * t + E], ACT.Exp,
                                               bias=small[:, 4, t, 0:1], accum_out=small[:, 4, t, 1:2])
                copied(ins, key)

            copy_job(("xT", 2), xT[:], bank(("xT", 2))[:, 0:T])
            gates("gate0", 1)
            copy_job("cw0T", cwT[:], bank("cw0T")[0:NE0, 0:T])
            for i in range(NE0):
                e = (i + E) % NE0
                act.wait_ge(h_filled, i + 1)
                if i >= 2:
                    act.wait_ge(h_dve, i - 1)
                for r in range(2):
                    ins = nc.scalar.activation(hid[:, i % 2, r, :], banks[:, 2 * (i % 2), T * r:T * r + T], ACT.Identity,
                                               bias=bcol[:, r, e:e + 1])
                ins.then_inc(h_act, 1)
                act.wait_ge(gate_ready, i + 1)
                if i >= 2:
                    act.wait_ge(a_ready, i - 1)
                nc.scalar.activation(hid[:, i % 2, 2, :], tmp[:, i % 2, :], ACT.Tanh, scale=1.702 / 2).then_inc(tanh_ready, 1)
            copy_job(("xT", 3), xT[:], bank(("xT", 3))[:, 0:T])
            for i in range(4):
                wait_filled(act, ("q1T", i))
                copied(nc.scalar.activation(oT[:, 2 * i:2 * i + 2, :].rearrange("p i t -> p (i t)"), bank(("q1T", i)), ACT.Copy,
                                            scale=HALF_H ** -0.5), ("q1T", i))
            for i in range(0, 8, 2):
                h = 4 * (i // 2) + i % 2
                copy_job(("qk", i), qk[:, :, h:h + 3:2, :].rearrange("p b h q -> p h b q"),
                         bank(("qk", i)).rearrange("p (h b q) -> p h b q", h=2, b=B))
            for i in range(B + 1):
                if i < B:
                    for g in range(G):
                        k = B * G + G * i + g
                        act.wait_ge(s_max, k + 1)
                        t = big[:, (i % 2) * G + g, :]
                        nc.scalar.activation(t, t, ACT.Exp, bias=nmax[:, k:k + 1], scale=-1.0,
                                             accum_out=rsum[:, k:k + 1]).then_inc(s_exp, 1)
                for key in FILL1[i]:
                    weight(key)
                if i >= 1:
                    for c in (0, 2, 4):
                        if i >= 2:
                            act.wait_ge(av_read, C * B + (C + 1) * (i - 2) + c + 1)
                        key = ("p1T", i - 1, c)
                        if c < C:
                            copy_job(key, pT[:, c, :], bank(key))
                        else:
                            r = Q * ((i - 1) % BT)
                            copy_job(key, pT[r:r + Q, c, :], bank(key)[0:Q, :])
            for i in (0, 2):
                copy_job(("o1T", i), oT[:, 2 * i:2 * i + 2, :].rearrange("p i t -> p (i t)"), bank(("o1T", i)))
            copy_job(("xT", 4), xT[:], bank(("xT", 4))[:, 0:T])
            copy_job(("xT", 5), xT[:], bank(("xT", 5))[:, 0:T])
            gates("gate1", 2)
            copy_job("cw1T", cwT[:], bank("cw1T")[0:NE0, 0:T])
            for e in range(E):
                act.wait_ge(h_filled, NE0 + e + 1)
                if e >= 2:
                    wait_filled(act, ("y1", e - 2))
                for k in range(2):
                    ins = nc.scalar.activation(hid[:, e % 2, k, :], banks[:, 2 * (e % 2), T * k:T * k + T], ACT.Relu,
                                               bias=cols[:, 22 + KH * e + k:23 + KH * e + k])
                ins.then_inc(h_act, 1)

        @block.vector
        def _(dve):
            n = 0

            def step(ins):
                nonlocal n
                n += 1
                ins.then_inc(dve_step, 1)
                dve.wait_ge(dve_step, n)

            def copy_job(key, dst, src):
                wait_filled(dve, key)
                copied(nc.vector.tensor_copy(dst, src), key)

            def layer_norm(k, src, at, dst):
                for t in range(NT):
                    ins = nc.vector.bn_stats(stats[:, at + t, :], src[:, t, :])
                step(ins)
                for t in range(NT):
                    ins = nc.vector.bn_aggr(mv[:, at + t, :], stats[:, at + t, :])
                step(ins)
                nc.vector.tensor_scalar(rstd[:, at:at + NT], mv[:, at:at + NT, 1], LN_EPS, None, ALU.add).then_inc(ln_var, 1)
                dve.wait_ge(ln_rstd, k)
                for t in range(NT):
                    ins = nc.vector.tensor_scalar(dst[:, t, :], src[:, t, :], mv[:, at + t, 0:1], rstd[:, at + t:at + t + 1],
                                                  ALU.subtract, ALU.mult)
                return ins

            dve.wait_ge(x_loaded, 16)
            layer_norm(1, x_sb, 32, xln).then_inc(ln_done, 1)

            dve.wait_ge(consts_ready, 1)
            step(nc.vector.tensor_reduce(mask4[:], sel16[:].rearrange("p (g j) -> p j g", j=4), AX, ALU.add))
            nc.vector.tensor_scalar(mask4s[:], mask4[:], float(8.0 ** -0.5), None, ALU.mult)
            nc.vector.tensor_reduce(mask2[:], sel4[:].rearrange("p (h s) -> p h s", s=2), AX, ALU.add)
            nc.vector.tensor_reduce(causal[:], caus3[:].rearrange("p j k -> p k j"), AX, ALU.add)
            nc.vector.tensor_tensor(half_a[:], sel4[:, 0:1], sel4[:, 2:3], ALU.add)
            nc.vector.scalar_tensor_tensor(half_b[:], sel4[:, 1:2], -1.0, sel4[:, 3:4], ALU.mult, ALU.subtract)
            step(nc.vector.reciprocal(icnt[:], icnt[:]))

            def make_qblk(dst, src, count):
                return nc.vector.tensor_tensor(
                    dst, broadcast(src.rearrange("p (b q) -> p b q", q=Q), 2, HG),
                    broadcast(broadcast(mask4s[:], 1, count), 3, Q), ALU.mult)

            wait_copied(dve, "q0T")
            make_qblk(qblk_c, qT[:], B).then_inc(qblk_ready, 1)

            def v_copy(b):
                copy_job(("v0", b), v0[:, b].rearrange("p c d -> p (c d)"), bank(("v0", b)))

            def ctx_stats(b):
                dve.wait_ge(ctx_loaded[b], 16)
                cs = slice(C * b, C * b + C)
                for c in range(C):
                    ins = nc.vector.bn_stats(stats[:, C * b + c, :], ctx_sb[:, b, c, :])
                step(ins)
                for c in range(C):
                    ins = nc.vector.bn_aggr(mv[:, C * b + c, :], stats[:, C * b + c, :])
                step(ins)
                nc.vector.tensor_scalar(nmr[:, cs], mv[:, cs, 0], -1.0, None, ALU.mult)
                nc.vector.tensor_scalar(rstd[:, cs], mv[:, cs, 1], LN_EPS, None, ALU.add).then_inc(cstat_ready, 1)

            def weight(key):
                kind, e = key[0], key[-1]
                if kind in ON_ACT:
                    return
                if kind == "w13T":
                    copy_job(key, w13T[:, e].rearrange("p f i -> p (f i)"), bank(key))
                if kind == "w2T":
                    m = min(4, NE0 - 4 * e)
                    wait_filled(dve, key)
                    copied(nc.vector.tensor_scalar(w2T[:, 4 * e:4 * e + m, :].rearrange("p e d -> p (e d)"), bank(key)[:, 0:P * m],
                                                   0.5, None, ALU.mult), key)
                if kind == "m12":
                    copy_job(key, m12[:], bank(key)[:, 0:P])
                    dve.wait_ge(bc_loaded, 16 * 8)
                    wait_copied(dve, "rowsT")
                    nc.vector.scalar_tensor_tensor(uu[:, 64:65], cols[:, 4:5], alpha[:, 0:1], cols[:, 3:4], ALU.mult, ALU.add)
                    nc.vector.tensor_scalar(uu[:, 32:64], uu[:, 32:64], alpha[:, 0:1], None, ALU.mult).then_inc(uu_ready, 1)
                if kind == "woT":
                    copy_job(key, woT[:], bank(key)[:, 0:P])
                if kind == "g":
                    copy_job(key, gl[:], bank(key)[0:65, 0:P])
                if kind == "wkT":
                    copy_job(key, wkT[:, 4 * e:4 * e + 4, :].rearrange("p i d -> p (i d)"), bank(key))

            for b in range(2):
                ctx_stats(b)
                v_copy(b)

            def invert_sums(i, b):
                dve.wait_ge(s_exp, i + G)
                nc.vector.reciprocal(rinv[:, i:i + G], rsum[:, i:i + G]).then_inc(s_rinv, 1)

            for i in range(B + 1):
                if i < B:
                    for g in range(G):
                        k = G * i + g
                        dve.wait_ge(s_filled, k + 1)
                        nc.vector.tensor_reduce(nmax[:, k:k + 1], banks[:, g, :], AX, ALU.max, negate=True).then_inc(s_max, 1)
                for key in FILL[i]:
                    weight(key)
                if i + 2 < B:
                    ctx_stats(i + 2)
                    v_copy(i + 2)
                if i >= 1:
                    for c in (1, 3):
                        if i >= 2:
                            dve.wait_ge(av_read, C * (i - 2) + c + 1)
                        copy_job(("p0T", i - 1, c), pT[:, c, :], bank(("p0T", i - 1, c)))
                if i < B:
                    invert_sums(G * i, i)
                if i in (BT, B):
                    t = i // BT - 1
                    dve.wait_ge(av_read, C * BT * (t + 1))
                    step(nc.vector.tensor_tensor(own.rearrange("p (b q j) -> p b j q", b=BT, j=HG),
                                                 acc.rearrange("p (b j q) -> p b j q", b=BT, j=HG),
                                                 broadcast(broadcast(mask4[:], 1, BT), 3, Q), ALU.mult))
                    step(nc.vector.tensor_reduce(oT[:, 0, P * t:P * t + P], own.rearrange("p (t j) -> p t j", j=HG), AX, ALU.add))
                    nc.vector.tensor_scalar(oT[:, 0, P * t:P * t + P], oT[:, 0, P * t:P * t + P], cols[:, 2:3], None,
                                            ALU.add).then_inc(o0T_ready, 1)

            def add_to_x(key, base):
                wait_filled(dve, key)
                ins = nc.vector.tensor_tensor(x_sb[:], bank(key)[:, 0:T].rearrange("p (t d) -> p t d", t=NT), base[:], ALU.add)
                copied(ins, key)
                wait_copied(dve, key)

            dve.wait_ge(bias_added, 1)
            add_to_x("o0", xb_sb)

            layer_norm(2, x_sb, 34, xln).then_inc(ln_done, 1)
            dve.wait_ge(self_loaded, 16 * 12)
            lam_v = lam_in.rearrange("p i g d -> p i (g d)")
            nc.vector.tensor_tensor(lam_v[:, 0, :], lam_v[:, 0, :], lam_v[:, 1, :], ALU.mult)
            step(nc.vector.tensor_tensor(lam_v[:, 2, :], lam_v[:, 2, :], lam_v[:, 3, :], ALU.mult))
            nc.vector.tensor_reduce(small[:, 1, 0, 0:8], lam_in[:, 0], AX, ALU.add)
            nc.vector.tensor_reduce(small[:, 2, 0, 0:8], lam_in[:, 2], AX, ALU.add).then_inc(lam_sum, 1)
            for i in range(2):
                ins = nc.vector.tensor_scalar(wso[:, i, :], wso[:, i, :], cols[:, 5:6], 0.2, ALU.mult, ALU.mult)
            ins.then_inc(wso_ready, 1)
            dve.wait_ge(lam_exp, 1)
            step(nc.vector.tensor_tensor(lam_c[:], small[:, 1, 0, 0:8], small[:, 2, 0, 0:8], ALU.subtract))
            step(nc.vector.tensor_scalar(lam_c[:], lam_c[:], 0.8, None, ALU.add))
            step(nc.vector.tensor_scalar(lam_c[:], lam_c[:], half_b[:, 0:1], half_a[:, 0:1], ALU.mult, ALU.add))

            wait_filled(dve, "qd")
            copied(make_qblk(qblk_d, bank("qd"), 2 * B), "qd")
            for i in range(4):
                wait_filled(dve, ("vd", i))
                ins = nc.vector.tensor_tensor(vblk[:, 16 * i:16 * i + 16], bank(("vd", i)).rearrange("p (n h d) -> p n h d", h=2, d=16),
                                              broadcast(broadcast(mask2[:], 1, 16), 3, 16), ALU.mult)
                copied(ins, ("vd", i))
            for i in range(4):
                dve.wait_ge(d_filled, i + 1)
                sc = big[:, i, 0:S].rearrange("p (n k) -> p n k", k=Q)
                step(nc.vector.tensor_tensor(sc, banks[:, i, :].rearrange("p (n k) -> p n k", k=Q),
                                             broadcast(causal[:], 1, 16), ALU.add))
                step(nc.vector.tensor_reduce(nmax[:, 16 * (i % 4):16 * (i % 4) + 16], sc, AX, ALU.max))
                nc.vector.tensor_tensor(sc, sc, broadcast(nmax[:, 16 * i:16 * i + 16], 2, Q), ALU.subtract).then_inc(d_sub, 1)
            for i in range(4):
                dve.wait_ge(d_exp, i + 1)
                sc = big[:, i, 0:S].rearrange("p (n k) -> p n k", k=Q)
                rs = slice(16 * i, 16 * i + 16)
                step(nc.vector.tensor_reduce(rsum[:, rs], sc, AX, ALU.add))
                step(nc.vector.reciprocal(rinv[:, rs], rsum[:, rs]))
                step(nc.vector.tensor_tensor(rinv[:, rs].rearrange("p (b h) -> p b h", h=2), rinv[:, rs].rearrange("p (b h) -> p b h", h=2),
                                             broadcast(lam_c[:, i:i + 5:4], 1, B), ALU.mult))
                step(nc.vector.tensor_tensor(sc, sc, broadcast(rinv[:, rs], 2, Q), ALU.mult))
                nc.vector.transpose(pT[:, i, :], big[:, i, 0:S]).then_inc(d_pT, 1)
            dve.wait_ge(d_sq, 1)
            ms = small[:, 0].rearrange("p t h -> p (t h)")
            step(nc.vector.tensor_reduce(ms, tmp[:, 0:2, :].rearrange("p t f -> p (t f)").rearrange("p (n d) -> p n d", d=16), AX, ALU.add))
            nc.vector.tensor_scalar(ms, ms, 1.0 / 16, LN_EPS, ALU.mult, ALU.add).then_inc(d_ms, 1)
            dve.wait_ge(d_rms, 1)
            nc.vector.tensor_tensor(tmp[:, 0:2, :].rearrange("p t f -> p (t f)").rearrange("p (n d) -> p n d", d=16),
                                    acc.rearrange("p (n d) -> p n d", d=16), broadcast(ms, 2, 16), ALU.mult).then_inc(d_on, 1)
            add_to_x("od", x_sb)

            layer_norm(3, x_sb, 36, xln).then_inc(ln_done, 1)

            def combine_weights(key, k, bias):
                wait_filled(dve, key)
                lg = bank(key)[:, 0:2 * E].rearrange("p (t e) -> p t e", t=NT)
                nc.vector.tensor_reduce(small[:, 4, :, 0], lg, AX, ALU.max, negate=True).then_inc(g_max, 1)
                wait_copied(dve, key)
                step(nc.vector.reciprocal(small[:, 5, :, 0:1], small[:, 4, :, 1:2]))
                step(nc.vector.tensor_tensor(small[:, 3, :, 0:E], small[:, 3, :, 0:E], small[:, 5, :, 0:1].to_broadcast([P, NT, E]), ALU.mult))
                ranked = small[:, 3, :, 0:E]
                if bias is not None:
                    step(nc.vector.tensor_tensor(small[:, 6, :, 0:E], ranked, broadcast(bias, 1, NT), ALU.add))
                    ranked = small[:, 6, :, 0:E]
                for t in range(NT):
                    ins = nc.vector.max(m8[:, t, :], ranked[:, t])
                step(ins)
                for t in range(NT):
                    ins = nc.vector.max_index(ix[:, t, :], m8[:, t, :], ranked[:, t])
                step(ins)
                step(nc.vector.tensor_copy(small[:, 7, :, 0:E], ix[:]))
                for t in range(NT):
                    ins = nc.vector.tensor_scalar(small[:, 8, t, 0:E], iota8[:], small[:, 7, t, 0:1], None, ALU.is_equal)
                step(ins)
                for t in range(NT):
                    ins = nc.vector.scalar_tensor_tensor(small[:, 9, t, 0:E], iota8[:], small[:, 7, t, 1:2], small[:, 8, t, 0:E],
                                                         ALU.is_equal, ALU.add)
                step(ins)
                ins = nc.vector.tensor_tensor(cw[:, :, 0:E], small[:, 9, :, 0:E], small[:, 3, :, 0:E], ALU.mult)
                if bias is None:
                    step(ins)
                    step(nc.vector.tensor_reduce(small[:, 10, :, 0], cw[:, :, 0:E], AX, ALU.add))
                    step(nc.vector.reciprocal(small[:, 10, :, 1:2], small[:, 10, :, 0:1]))
                    ins = nc.vector.tensor_tensor(cw[:, :, 0:E], cw[:, :, 0:E], small[:, 10, :, 1:2].to_broadcast([P, NT, E]), ALU.mult)
                ins.then_inc(cw_ready, 1)
                dve.wait_ge(cw_ready, k)

            combine_weights("gate0", 1, gb[:])
            s = 0

            def combine(key, e, weights):
                wait_filled(dve, key)
                y = bank(key)[:, 0:T].rearrange("p (t d) -> p t d", t=NT)
                if weights is None:
                    ins = nc.vector.tensor_tensor(x_sb[:], y, x_sb[:], ALU.add)
                else:
                    for t in range(NT):
                        ins = nc.vector.scalar_tensor_tensor(x_sb[:, t, :], y[:, t, :], weights[:, t, e:e + 1], x_sb[:, t, :],
                                                             ALU.mult, ALU.add)
                copied(ins, key)
                wait_copied(dve, key)

            for i in range(NE0 + 1):
                if i < NE0:
                    e = (i + E) % NE0
                    dve.wait_ge(h_act, i + 1)
                    if i >= 2:
                        dve.wait_ge(lin_ready, i - 1)
                        dve.wait_ge(tanh_ready, i - 1)
                    for r in range(2):
                        ins = nc.vector.scalar_tensor_tensor(tmp[:, 2 * r + i % 2, :], banks[:, 2 * (i % 2) + 1, T * r:T * r + T],
                                                             bcol[:, r, NE0 + e:NE0 + e + 1], hid[:, i % 2, r, :], ALU.add, ALU.mult)
                    ins.then_inc(h_dve, 1)
                    dve.wait_ge(h_dve, i + 1)
                    nc.vector.tensor_scalar(tmp[:, i % 2, :], tmp[:, i % 2, :], 7.0, None, ALU.min).then_inc(gate_ready, 1)
                    dve.wait_ge(gate_ready, i + 1)
                    dve.wait_ge(lin_ready, i + 1)
                    step(nc.vector.scalar_tensor_tensor(tmp[:, 4 + i % 2, :], tmp[:, 4 + i % 2, :], 1.0, tmp[:, i % 2, :], ALU.add, ALU.mult))
                    dve.wait_ge(tanh_ready, i + 1)
                    if i >= 2:
                        wait_filled(dve, ("y0", i - 2))
                    nc.vector.scalar_tensor_tensor(hid[:, i % 2, 3, :], hid[:, i % 2, 2, :], 1.0, tmp[:, 4 + i % 2, :],
                                                   ALU.add, ALU.mult).then_inc(a_ready, 1)
                if i >= 1:
                    e = (i - 1 + E) % NE0
                    combine(("y0", i - 1), e, None if e == E else cw)

            step(layer_norm(4, x_sb, 38, xln))
            step(layer_norm(5, xln, 38, lat))
            step(nc.vector.tensor_tensor(lat[:], lat[:], broadcast(bc[:, 4, :], 1, NT), ALU.mult))
            nc.vector.tensor_tensor(lat[:], lat[:], broadcast(bc[:, 5, :], 1, NT), ALU.add).then_inc(ln_done, 1)
            for i in range(1, 8, 2):
                h = 4 * (i // 2) + i % 2
                copy_job(("qk", i), qk[:, :, h:h + 3:2, :].rearrange("p b h q -> p h b q"),
                         bank(("qk", i)).rearrange("p (h b q) -> p h b q", h=2, b=B))
            dve.wait_ge(negmask_ready, 1)
            first = B * G
            for i in range(B + 1):
                if i < B:
                    for g in range(G):
                        k = first + G * i + g
                        dve.wait_ge(s_filled, k + 1)
                        if i >= 2:
                            wait_filled(dve, ("p1T", i - 2, C))
                        pair = banks[:, 2 * (g % 2):2 * (g % 2) + 2, :].rearrange("p a s -> p (a s)")[:, 0:SL]
                        nc.vector.tensor_tensor_reduce(out=big[:, (i % 2) * G + g, :], in0=pair, in1=negmask[:, i, :], scale=-1.0,
                                                       scalar=3.0e38, op0=ALU.add, op1=ALU.min,
                                                       accum_out=nmax[:, k:k + 1]).then_inc(s_max, 1)
                for key in FILL1[i]:
                    weight(key)
                if i >= 1:
                    for c in (1, 3):
                        if i >= 2:
                            dve.wait_ge(av_read, C * B + (C + 1) * (i - 2) + c + 1)
                        copy_job(("p1T", i - 1, c), pT[:, c, :], bank(("p1T", i - 1, c)))
                if i < B:
                    invert_sums(first + G * i, B + i)
                if i >= 1:
                    dve.wait_ge(av_read, C * B + (C + 1) * i)
                    nc.vector.tensor_copy(yT[:, :, Q * (i - 1):Q * i], acc.rearrange("p (h q) -> p h q", q=Q)).then_inc(acc_read, 1)
            for i in (1, 3):
                copy_job(("o1T", i), oT[:, 2 * i:2 * i + 2, :].rearrange("p i t -> p (i t)"), bank(("o1T", i)))
            dve.wait_ge(bias_added, 2)
            add_to_x("o1", xb_sb)

            layer_norm(6, x_sb, 32, xln).then_inc(ln_done, 1)
            flat_bq = "p b q -> p (b q)"
            nc.vector.memset(scan[64:65, 0, :], 1.0)
            wait_filled(dve, "z")
            step(nc.vector.tensor_tensor_scan(scan[32:64, 1, :], keep[32:64].rearrange(flat_bq), bank("z")[32:64, 0:T], 0.0, ALU.mult, ALU.add))
            wait_filled(dve, "ac")
            step(nc.vector.tensor_tensor_scan(scan[0:64, 2, :], keep[:].rearrange(flat_bq), bank("ac")[0:64, T:2 * T], 0.0, ALU.mult, ALU.add))
            copied(nc.vector.tensor_tensor(scan[32:64, 1, :], scan[32:64, 1, :], icnt[32:64].rearrange(flat_bq), ALU.mult), "z")
            wait_copied(dve, "z")
            copied(nc.vector.tensor_tensor(scan[0:64, 0, :], bank("ac")[0:64, 0:T], scan[0:64, 2, :], ALU.mult), "ac")
            wait_copied(dve, "ac")
            step(nc.vector.tensor_tensor(scan[32:64, 0, :], scan[32:64, 0, :], scan[32:64, 1, :], ALU.mult))
            nc.vector.tensor_tensor(scan[0:64, 0, :], scan[0:64, 0, :], icnt[:].rearrange(flat_bq), ALU.mult).then_inc(pr_ready, 1)
            add_to_x("ol", x_sb)

            layer_norm(7, x_sb, 34, xln).then_inc(ln_done, 1)
            combine_weights("gate1", 2, None)
            for e in range(E + 1):
                if e < E:
                    dve.wait_ge(h_filled, NE0 + e + 1)
                    if e >= 2:
                        wait_filled(dve, ("y1", e - 2))
                    for k in range(2, 4):
                        b1c = cols[:, 22 + KH * e + k:23 + KH * e + k]
                        ins = nc.vector.tensor_scalar(hid[:, e % 2, k, :], banks[:, 2 * (e % 2) + 1, T * (k - 2):T * (k - 1)],
                                                      b1c, 0.0, ALU.add, ALU.max)
                    ins.then_inc(h_dve, 1)
                if e >= 1:
                    combine(("y1", e - 1), e - 1, cw)
            wait_filled(dve, "b1y")
            nc.vector.tensor_tensor(x_sb[:], bank("b1y")[:, 0:T].rearrange("p (t d) -> p t d", t=NT), x_sb[:], ALU.add).then_inc(x_final, 1)

        @block.tensor
        def _(pe):
            def mm(dst, lhsT, rhs, start=True, stop=True, at=None):
                return nc.tensor.matmul(dst, lhsT, rhs, start=start, stop=stop, tile_position=at)

            def tr(dst, src):
                k = src.shape[0]
                return nc.tensor.transpose(dst, src, ident[0:k, 0:k])

            pe.wait_ge(ident_ready, 1)
            pe.wait_ge(w0_loaded, 64)
            for i in range(4):
                ins = tr(bank("w0T")[:, P * i:P * i + P], w0raw[:, i, :])
            filled(ins, "w0T")
            pe.wait_ge(rows_loaded, 16 * 13)
            filled(tr(bank("rowsT")[:, 0:ROWS], rows), "rowsT")
            for r in range(2):
                ins = tr(bank("bias0T")[:, 2 * NE0 * r:2 * NE0 * r + 2 * NE0], brow.rearrange("n (i r) -> n r i", r=2)[:, r, :])
            filled(ins, "bias0T")

            def x_transposes(i, src):
                key = ("xT", i)
                pe.wait_ge(ln_done, i + 1)
                wait_bank_free(pe, key)
                for t in range(NT):
                    ins = tr(bank(key)[:, P * t:P * t + P], src[:, t, :])
                filled(ins, key)
                wait_copied(pe, key)

            x_transposes(0, xln)
            wait_copied(pe, "w0T")
            wait_bank_free(pe, "q0T")
            filled(mm(bank("q0T")[:, 0:T], w0T[:, 0, :], xT[:]), "q0T")

            def ctx_transposes(b):
                key = ("ctxT", b)
                pe.wait_ge(ctx_loaded[b], 16)
                wait_bank_free(pe, key)
                for c in range(C):
                    ins = tr(bank(key)[:, P * c:P * c + P], ctx_sb[:, b, c, :])
                filled(ins, key)

            def keys_values(b):
                wait_copied(pe, ("ctxT", b))
                wait_bank_free(pe, ("k0T", b))
                filled(mm(bank(("k0T", b)), w0T[:, 1, :], ctxT[:, b].rearrange("p c k -> p (c k)")), ("k0T", b))
                wait_bank_free(pe, ("v0", b))
                for c in range(C):
                    ins = mm(bank(("v0", b))[:, P * c:P * c + P], ctxT[:, b, c, :], w0T[:, 2, :])
                filled(ins, ("v0", b))

            def weight(key):
                kind, e = key[0], key[-1]
                wait_bank_free(pe, key)
                bk = bank(key)
                if kind == "w13T":
                    pe.wait_ge(exp0_loaded[e // 4 if e < E else 1], 32 if e < 4 else 64)
                    for w in range(2):
                        for r in range(2):
                            src = shared_raw[:, 2 * w + r, :] if e == E else w1raw0[:, w, 2 * e + r, :]
                            ins = tr(bk[:, P * (2 * w + r):P * (2 * w + r + 1)], src)
                if kind == "w2T":
                    pe.wait_ge(exp0_w2_loaded, 16 * 2)
                    for m in range(min(4, NE0 - 4 * e)):
                        ins = tr(bk[:, P * m:P * m + P], w2raw[:, 4 * e + m, :])
                if kind == "m12":
                    pe.wait_ge(lin_loaded, 16 * 10)
                    mm(bk[:, 0:64], wl[:, 0, :], lowr[:, 0:2, :].rearrange("p a r -> p (a r)"))
                    ins = mm(bk[:, 64:128], wl[:, 1, :], lowr[:, 2:4, :].rearrange("p a r -> p (a r)"))
                if kind == "woT":
                    ins = tr(bk[:, 0:P], wl[:, 2, :])
                if kind == "g":
                    pe.wait_ge(uu_ready, 1)
                    wait_copied(pe, ("woT",))
                    ins = mm(bk[0:65, 0:P], uu[:], woT[:])
                if kind == "xnT":
                    pe.wait_ge(xn_ready, e + 1)
                    for c in range(C):
                        ins = tr(bk[:, P * c:P * c + P], ctx_sb[:, e, c, :])
                if kind == "wkT":
                    pe.wait_ge(lat_loaded, 16 * 2)
                    for m in range(4):
                        ins = tr(bk[:, P * m:P * m + P], wkv1[:, P * (4 * e + m):P * (4 * e + m + 1)])
                if kind == "w11T":
                    pe.wait_ge(exp1_loaded[e % RAW_SLOTS], 16 * (e // RAW_SLOTS + 1))
                    for k in range(KH):
                        ins = tr(bk[:, P * k:P * k + P], wraw1[:, e % RAW_SLOTS, k, :])
                if kind == "w12T":
                    pe.wait_ge(exp1_loaded[e % RAW_SLOTS], 16 * (e // RAW_SLOTS + 3))
                    for k in range(KH):
                        ins = tr(bk[:, P * k:P * k + P], wraw1[:, e % RAW_SLOTS, k, :])
                filled(ins, key)

            for b in range(2):
                ctx_transposes(b)
                keys_values(b)
            pe.wait_ge(qblk_ready, 1)
            for i in range(B + 1):
                if i < B:
                    wait_copied(pe, ("k0T", i))
                    for g in range(G):
                        if i:
                            pe.wait_ge(s_exp, G * (i - 1) + g + 1)
                        r = slice(32 * g, 32 * g + 32)
                        mm(banks[:, g, :], qblk_c[r, i].rearrange("p j q -> p (j q)"), k0T[r, i, :],
                           at=(32 * g, 0)).then_inc(s_filled, 1)
                for key in FILL[i]:
                    weight(key)
                if i + 2 < B:
                    ctx_transposes(i + 2)
                    keys_values(i + 2)
                if i >= 1:
                    b = i - 1

                    def probs_transposes(c):
                        key = ("p0T", b, c)
                        if c == 0:
                            pe.wait_ge(p_ready, G * b + G)
                        wait_bank_free(pe, key)
                        for g in range(G):
                            ins = tr(bank(key)[:, P * g:P * g + P], big[:, (b % 2) * G + g, P * c:P * c + P])
                        filled(ins, key)

                    def attend(c):
                        wait_copied(pe, ("p0T", b, c))
                        if c == 0:
                            wait_copied(pe, ("v0", b))
                            if b == BT:
                                pe.wait_ge(o0T_ready, 1)
                        for g in range(G):
                            ins = mm(acc[32 * g:32 * g + 32, P * (b % BT):P * (b % BT) + P], v0[:, b, c, 32 * g:32 * g + 32],
                                     pT[:, c, P * g:P * g + P], start=c == 0, stop=c == C - 1, at=(0, 32 * g))
                        ins.then_inc(av_read, 1)
                        return ins

                    probs_transposes(0)
                    for c in range(1, C):
                        probs_transposes(c)
                        attend(c - 1)
                    attend(C - 1)

            def project(key, n_in, lhs, rhs):
                wait_bank_free(pe, key)
                for t in range(NT):
                    for k in range(n_in):
                        ins = mm(bank(key)[:, P * t:P * t + P], lhs(k, t), rhs(k), start=k == 0, stop=k == n_in - 1)
                return ins

            pe.wait_ge(o0T_ready, 2)
            filled(project("o0", 1, lambda k, t: oT[:, 0, P * t:P * t + P], lambda k: w0T[:, 3, :]), "o0")

            x_transposes(1, xln)
            pe.wait_ge(self_loaded, 16 * 12)
            for key, w in (("qd", 0), ("kd", 1)):
                wait_bank_free(pe, key)
                for m in range(2):
                    ins = mm(bank(key)[:, T * m:T * m + T], ws[:, w, P * m:P * m + P], xT[:])
                filled(ins, key)
            for i in range(4):
                wait_bank_free(pe, ("vd", i))
                for m in range(2):
                    b = 2 * i + m
                    ins = mm(bank(("vd", i))[:, T * m:T * m + T], x_rep[:, b].rearrange("p j q -> p (j q)"), ws[:, 2, :])
                filled(ins, ("vd", i))
            wait_copied(pe, "qd")
            wait_copied(pe, "kd")
            for g in range(G):
                r = slice(32 * g, 32 * g + 32)
                for b in range(B):
                    for half in range(2):
                        col = (b * 2 + half) * Q
                        ins = mm(banks[:, g, col:col + Q], qblk_d[r, half * B + b].rearrange("p j q -> p (j q)"),
                                 kdT[r, half, Q * b:Q * b + Q], at=(32 * g, 0))
                ins.then_inc(d_filled, 1)
            wait_copied(pe, ("vd", 3))
            for g in range(G):
                pe.wait_ge(d_pT, g + 1)
                for b in range(B):
                    r = Q * (b % BT)
                    for half in range(2):
                        n = half * 4 + g
                        col = T * (b // BT) + 32 * n
                        ins = mm(acc[r:r + Q, col:col + 32], pT[:, g, (b * 2 + half) * Q:(b * 2 + half + 1) * Q],
                                 vblk[:, 8 * b + n].rearrange("p h d -> p (h d)"), at=(0, r))
            ins.then_inc(acc_filled, 1)
            pe.wait_ge(d_on, 1)
            for t in range(NT):
                wait_bank_free(pe, ("odT", t))
                for m in range(2):
                    ins = tr(bank(("odT", t))[:, P * m:P * m + P], tmp[:, t, P * m:P * m + P])
                filled(ins, ("odT", t))
            for t in range(NT):
                wait_copied(pe, ("odT", t))
            pe.wait_ge(wso_ready, 1)
            filled(project("od", 2, lambda k, t: oT[:, k, P * t:P * t + P], lambda k: wso[:, k, :]), "od")

            x_transposes(2, xln)

            def gate_logits(key, c0):
                wait_bank_free(pe, key)
                for t in range(NT):
                    ins = mm(bank(key)[:, E * t:E * t + E], xT[:, P * t:P * t + P], cols[:, c0:c0 + E])
                filled(ins, key)

            def cw_transposes(key, k):
                pe.wait_ge(cw_ready, k)
                wait_bank_free(pe, key)
                for t in range(NT):
                    ins = tr(bank(key)[0:NE0, P * t:P * t + P], cw[:, t, :])
                filled(ins, key)

            gate_logits("gate0", 6)

            def hidden0(i):
                e = (i + E) % NE0
                if i >= 2:
                    pe.wait_ge(h_dve, i - 1)
                for w in range(2):
                    for r in range(2):
                        ins = mm(banks[:, 2 * (i % 2) + w, T * r:T * r + T], w13T[:, e, 2 * w + r, :], xT[:])
                ins.then_inc(h_filled, 1)

            hidden0(0)
            hidden0(1)
            cw_transposes("cw0T", 1)
            pe.wait_ge(b2_loaded, 48)
            for i in range(NE0):
                e = (i + E) % NE0
                key = ("y0", i)
                pe.wait_ge(a_ready, i + 1)
                wait_bank_free(pe, key)
                for t in range(NT):
                    ins = mm(bank(key)[:, P * t:P * t + P], hid[:, i % 2, 3, P * t:P * t + P], w2T[:, e, :], stop=e != E)
                    if e == E:
                        wait_copied(pe, "cw0T")
                        ins = mm(bank(key)[:, P * t:P * t + P], cwT[:, P * t:P * t + P], b2x[:], start=False)
                filled(ins, key)
                if i + 2 < NE0:
                    hidden0(i + 2)

            x_transposes(3, lat)
            pe.wait_ge(wq1_loaded, 16)
            for i in range(4):
                wait_bank_free(pe, ("q1T", i))
                for m in range(2):
                    ins = mm(bank(("q1T", i))[:, T * m:T * m + T], wq1[:, P * (2 * i + m):P * (2 * i + m + 1)], xT[:])
                filled(ins, ("q1T", i))
            for i in range(8):
                a, m = i // 2, i % 2
                wait_copied(pe, ("q1T", a))
                wait_bank_free(pe, ("qk", i))
                r = slice(HALF_H * m, HALF_H * m + HALF_H)
                for j in range(2):
                    ins = mm(bank(("qk", i))[:, T * j:T * j + T], wkT[r, 2 * a + j, :], oT[r, 2 * a + j, :], at=(HALF_H * m, 0))
                filled(ins, ("qk", i))
            for i in range(5, 8):
                wait_copied(pe, ("qk", i))
            for i in range(B + 1):
                if i < B:
                    for g in range(G):
                        k = G * i + g
                        if k >= 2:
                            pe.wait_ge(s_max, B * G + k - 1)
                        w = qk[:, i, HG * g:HG * g + HG, :].rearrange("p h q -> p (h q)")
                        mm(banks[:, 2 * (g % 2), :], w, xnT[:, i, :])
                        mm(banks[:, 2 * (g % 2) + 1, 0:Q], w, xT[:, Q * i:Q * i + Q]).then_inc(s_filled, 1)
                for key in FILL1[i]:
                    weight(key)
                if i >= 1:
                    b = i - 1

                    def probs_transposes(c):
                        key = ("p1T", b, c)
                        if c == 0:
                            pe.wait_ge(p_ready, B * G + G * b + G)
                        wait_bank_free(pe, key)
                        m = P if c < C else Q
                        for g in range(G):
                            ins = tr(bank(key)[0:m, P * g:P * g + P], big[:, (b % 2) * G + g, P * c:P * c + m])
                        filled(ins, key)

                    def attend(c):
                        wait_copied(pe, ("p1T", b, c))
                        if c == 0 and b:
                            pe.wait_ge(acc_read, b)
                        if c < C:
                            return mm(acc, ctx_sb[:, b, c, :], pT[:, c, :], start=c == 0, stop=False).then_inc(av_read, 1)
                        r = slice(Q * (b % BT), Q * (b % BT) + Q)
                        return mm(acc, lat[r, b // BT, :], pT[r, c, :], start=False, stop=True, at=(Q * (b % BT), 0)).then_inc(av_read, 1)

                    probs_transposes(0)
                    for c in range(1, C + 1):
                        probs_transposes(c)
                        attend(c - 1)
                    attend(C)
            pe.wait_ge(acc_read, B)
            for i in range(4):
                wait_bank_free(pe, ("o1T", i))
                for m in range(2):
                    for h in range(HH):
                        head = HH * (2 * i + m) + h
                        ins = mm(bank(("o1T", i))[HALF_H * h:HALF_H * h + HALF_H, T * m:T * m + T],
                                 wkv1[:, 16 * HALF_H + HALF_H * head:16 * HALF_H + HALF_H * head + HALF_H],
                                 yT[:, head, :], at=(0, HALF_H * h))
                filled(ins, ("o1T", i))
            for i in range(1, 4):
                wait_copied(pe, ("o1T", i))
            filled(project("o1", 8, lambda k, t: oT[:, k, P * t:P * t + P], lambda k: wout1[:, k, :]), "o1")

            x_transposes(4, xln)
            wait_bank_free(pe, "ac")
            mm(bank("ac")[0:64, 0:T], m12[:, 0:64], xT[:])
            filled(mm(bank("ac")[0:64, T:2 * T], m12[:, 64:128], xT[:]), "ac")
            wait_bank_free(pe, "z")
            filled(mm(bank("z")[32:64, 0:T], lowr[:, 4, :], xT[:], at=(0, 32)), "z")
            pe.wait_ge(pr_ready, 1)
            filled(project("ol", 1, lambda k, t: scan[:, 0, P * t:P * t + P], lambda k: gl[:]), "ol")

            x_transposes(5, xln)
            gate_logits("gate1", 14)

            def hidden1(e):
                if e >= 2:
                    pe.wait_ge(h_act, NE0 + e - 1)
                    pe.wait_ge(h_dve, NE0 + e - 1)
                for k in range(KH):
                    ins = mm(banks[:, 2 * (e % 2) + k // 2, T * (k % 2):T * (k % 2) + T], w11T[:, e, k, :], xT[:])
                ins.then_inc(h_filled, 1)

            hidden1(0)
            hidden1(1)
            cw_transposes("cw1T", 2)
            for e in range(E):
                key = ("y1", e)
                pe.wait_ge(h_act, NE0 + e + 1)
                pe.wait_ge(h_dve, NE0 + e + 1)
                filled(project(key, KH, lambda k, t: hid[:, e % 2, k, P * t:P * t + P], lambda k: w12T[:, e, k, :]), key)
                if e + 2 < E:
                    hidden1(e + 2)
            wait_copied(pe, "cw1T")
            filled(project("b1y", 1, lambda k, t: cwT[0:E, P * t:P * t + P], lambda k: b2y[:]), "b1y")


def kernel(**inputs):
    import concourse.bacc as bacc
    from concourse.bass_utils import run_bass_kernel_spmd

    nc = bacc.Bacc("TRN2", target_bir_lowering=False, num_devices=1)
    arrays, d = {}, {}
    for name, value in inputs.items():
        a = np.ascontiguousarray(value)
        if a.ndim == 0:
            a = a.reshape(1)
        arrays["in_" + name] = a
        d[name] = nc.dram_tensor("in_" + name, a.shape, mybir.dt.from_np(a.dtype), kind="ExternalInput").ap()
    out = nc.dram_tensor("out_x", (B, Q, D), F32, kind="ExternalOutput").ap()
    build(nc, d, out)
    result = run_bass_kernel_spmd(nc, [arrays], core_ids=[0])
    return result.results[0]["out_x"]
```

```python
from contextlib import ExitStack

import numpy as np
import concourse.bass as bass
from concourse import mybir

F32 = mybir.dt.float32
BF16 = mybir.dt.bfloat16
U8 = mybir.dt.uint8
U32 = mybir.dt.uint32
ALU = mybir.AluOpType
ACT = mybir.ActivationFunctionType
AX = mybir.AxisListType.X

P = 128
D = 128
B = 8
Q = 32
T = B * Q
NT = T // P
BT = B // NT
S = 512
C = S // P
G = 4
HG = 4
HALF_H = 64
E = 8
NE0 = E + 1
KH = 4
SL = S + Q
NEG = -float(2.0 ** 127)
LN_EPS = 1e-5
RING = 3
ROWS = 54
KV = 4
CT = 2
RAW_SLOTS = 4


NEXT = {"heads0": 1.79, "out0": 1.2, "ln": 1.09, "xT": 1.29, "dproj": 2.05, "dval": 1.73, "dscore": 1.6,
        "dsoft": 2.07, "dprob": 4.11, "daT": 0.88, "dpv": 1.5, "drms": 4.56, "doT": 0.72, "dout": 1.09,
        "gate0": 1.44, "cwT0": 0.35, "lat": 1.42, "q1": 1.59, "qk": 0.86, "oT1": 2.3, "out1": 2.06, "lin": 5.16,
        "linout": 1.0, "gate1": 0.96}
LAG = {"lam_dots": (0, 0.6, 0, 0), "prep": (0, 0.94, 1.38, 0.95), "scores0": (0, 1.8, 1.02, 0),
       "norm0": (0, 0, 0, 0.38), "attend0": (0, 0.62, 0.74, 0), "xnT": (0, 0.78, 0, 0), "lat1": (0, 0, 0.83, 0),
       "scores1": (0, 2.01, 1.11, 0), "norm1": (0, 0, 0, 0.4), "attend1": (0, 0.7, 0.63, 0),
       "weight": (0, 0.79, 0.71, 0), "out0": (0, 0, 0.75, 0), "ln": (0, 0, 0, 1.07), "xT": (0.7, 0.66, 0, 0),
       "lat": (0.5, 0.83, 0, 0), "dproj": (0, 0.26, 0.8, 0), "dval": (0, 0, 1.02, 0), "dscore": (0, 0, 0, 0),
       "dsoft": (0, 1.9, 0, 0), "daT": (0, 0.6, 0, 0), "dpv": (0, 1.0, 0, 0), "drms": (0, 0, 0, 0.48),
       "doT": (0.28, 0.67, 0, 0), "dout": (0, 0, 0.5, 0), "gate0": (0, 0.57, 0.3, 0), "gate1": (0, 0.54, 0.05, 0),
       "cwT0": (0, 0.18, 0, 0), "cwT1": (0, 0.44, 0, 0), "hid0": (0, 0.93, 1.39, 1.86), "act0": (0, 0, 2.2, 0),
       "y0": (0, 0, 0.52, 0), "q1": (0, 0.92, 0, 0), "qk": (0, 0.68, 0.5, 0), "oT1": (0, 1.46, 2.05, 0),
       "out1": (0, 0, 0.7, 0), "lin": (0, 0, 0.69, 0), "linout": (0, 0, 0.5, 0), "hid1": (0, 0.9, 0.77, 0),
       "y1": (0, 0, 0.55, 0), "b1": (0, 0, 0.29, 0)}
PE, ACTE, DVE, POOL = range(4)
BATCH0 = (11.0, 14.4)
BATCH1 = (14.0, 13.66)
ATTEND0, ATTEND1 = 4.6, 4.14
CHUNK0, CHUNK1 = 0.29, 0.16
EXPERT0, EXPERT1, EXPERT1_LAST = 2.3, 3.54, 2.24
ACT0, Y0, Y1 = 2.42, 7.45, 2.66
WEIGHTS1 = (0.0, -10.0)
NUDGE = {('attend0', 0, 0): 2.3, ('attend0', 4, 2): 1.1, ('attend1', 3, 1): -1.5, ('cstat', 2): 1.6, ('dpv', 1): 1.9,
         ('gate1', 0): 1.3, ('hid1', 0, 4): -1.4, ('ln', 1, 1): -0.4, ('oT1', 1, 1): -1.7, ('scores1', 4, 1): 0.3,
         ('scores1', 4, 2): 3.4, ('scores1', 5, 2): -2.4, ('scores1', 6, 2): -3.3}
TAIL0 = 0.74
SHIFT = {"attend0": (-0.7, 0.0), "attend1": (-0.53, 0.0), "norm1": (0.0, 0.33), "xnT": (0.87, 0.0),
         "lat1": (-0.39, 0.0), "mask": (-0.23, -0.56), "heads0": (-0.01, -0.2), "dval": (-1.0, -1.81),
         "drms": (0.0, 0.17), "doT": (-0.02, -0.14), "gate0": (-0.24, 0.04), "q1": (-0.65, 0.17),
         "best0": (0.0, -0.81), "hid0": (0.0, 0.1), "act0": (-0.59, 0.0), "hid1": (0.49, 0.0), "y1": (0.0, 0.67),
         "cwT1": (0.99, -0.97)}
SLACK = (1.0, 1.0, 1.01, 0.65)
NORM0_AT, NORM1_AT = 2.4, 2.21
PREP_AT, WEIGHTS0_AT = 0.2, 0.03
LAT1_AT, XNT_AT = -0.8, -4.87
SELF0_AT = (0.8, 0.79)
CROSS1_AT = (0.96, 1.21)
DVE_CHUNKS = (((1, 3), (1, 3)), ((3,), (3,)))


def chain(at, slack, *steps):
    out = []
    for block_ in steps:
        out.append((at, block_))
        at += slack * NEXT[block_[0]]
    return out, at


def cross0(at, b, fills):
    period = BATCH0[b // BT]
    out = [(at + period * g / G, ("scores0", b, g)) for g in range(G)]
    out.append((at + period * 3 / G + NORM0_AT, ("norm0", b)))
    out += [(at + period + ATTEND0 + CHUNK0 * period * c, ("attend0", b, c)) for c in range(C + 1)]
    if b + 2 < B:
        out += [(at + period * (k + 0.3) / 3 + PREP_AT, ("prep", b + 2, k)) for k in range(3)]
    if b == BT - 1:
        out += [(at + period * 0.6, ("lam_dots",)), (at + period * 0.9, ("lam_end",))]
    if b < BT:
        out += [(at + period * 0.1, ("cstat", b))] + [(at + period * (k + 0.5) / G, ("cnorm", b, k)) for k in range(3)]
    else:
        out.append((at + period * 0.5, ("mask", b - BT)))
    return out + [(at + period * (k + 0.8) / len(fills) + WEIGHTS0_AT, ("weight", *f)) for k, f in enumerate(fills)]


def cross1(at, b):
    period = BATCH1[b // BT]
    out = [(at + XNT_AT, ("xnT", b)), (at + LAT1_AT, ("lat1", b))] + [(at + period * g / G, ("scores1", b, g)) for g in range(G)]
    out.append((at + period * 3 / G + NORM1_AT, ("norm1", b)))
    out += [(at + period + ATTEND1 + CHUNK1 * period * c, ("attend1", b, c)) for c in range(C + 2)]
    if b < BT:
        out += [(at + period * 0.1, ("cstat", BT + b))] + [(at + period * (k + 0.5) / G, ("cnorm", BT + b, k)) for k in range(3)]
    return out


def self0(at, t):
    out, at = chain(at, SLACK[t], ("heads0", t), ("out0", t), ("ln", 1, t), ("xT", 1, t), ("dproj", t), ("dval", t), ("dscore", t), ("dsoft", t, 0),
                    ("dsoft", t, 1), ("dprob", t, 0), ("dprob", t, 1), ("daT", t), ("dpv", t), ("drms", t), ("doT", t), ("dout", t),
                    ("ln", 2, t), ("xT", 2, t), ("gate0", t))
    out += [(at + 1.0, ("best0", t)), (at + 3.2, ("cwT0", t))]
    for i in range(NE0):
        out += [(at + EXPERT0 * i, ("hid0", t, i)), (at + EXPERT0 * i + ACT0, ("act0", t, i)), (at + EXPERT0 * i + Y0, ("y0", t, i))]
    tail, end = chain(at + EXPERT0 * (NE0 - 1) + Y0 + TAIL0, SLACK[t], ("ln", 3, t), ("ln", 4, t), ("lat", t), ("q1", t, 0), ("q1", t, 1),
                      *(("qk", t, n) for n in range(4)))
    return out + tail, end


def linear1(at, t, expert):
    out, at = chain(at, SLACK[2 + t], ("oT1", t, 0), ("oT1", t, 1), ("out1", t), ("ln", 5, t), ("xT", 5, t), ("lin", t), ("linout", t),
                    ("ln", 6, t), ("xT", 6, t), ("gate1", t))
    out += [(at + 1.4, ("best1", t)), (at + 3.4, ("cwT1", t))]
    for e in range(E):
        out += [(at + expert * e, ("hid1", t, e)), (at + expert * e + Y1, ("y1", t, e))]
    at += expert * E + Y1
    return out + [(at, ("b1", t)), (at + 0.5, ("store", t))]


def shift(block_):
    kind, *a = block_
    tile = a[0] if a and isinstance(a[0], int) else 0
    if kind in ("scores0", "attend0", "norm0", "prep", "scores1", "attend1", "norm1", "xnT", "lat1", "cstat", "cnorm"):
        tile = tile // BT
    return SHIFT.get(kind, (0.0, 0.0))[min(tile, 1)] + NUDGE.get(block_, 0.0)


def plan():
    w0 = [[("w2T", 0), ("w2T", 1), ("w2T", 2)], [("w13T", 0), ("w13T", 1), ("w13T", 8)],
          [("w13T", 2), ("w13T", 3), ("w13T", 4)], [("w13T", 5), ("w13T", 6), ("w13T", 7)],
          [("m12", 0), ("woT", 0), ("g", 0)], [("wkT", 0), ("wkT", 1)], [], []]
    experts1 = [("w11T", e) for e in range(E)] + [("w12T", e) for e in range(E)]
    out = [(-20.0, ("start",)), (0.2, ("rows",))] + [(-8.0 + 4 * b + k, ("prep", b, k)) for b in range(2) for k in range(3)]
    start0 = [BATCH0[0] * min(b, BT) + BATCH0[1] * max(b - BT, 0) for b in range(B + 1)]
    for b in range(B):
        out += cross0(start0[b], b, w0[b])
    first, latents_done = self0(max(at for at, b in out if b[0] == "attend0" and b[1] == BT - 1) + SELF0_AT[0], 0)
    experts_done = max(at for at, b in first if b[0] == "hid0") + 3.0
    scored = next(at for at, b in self0(0.0, 1)[0] if b[0] == "dscore")
    attended = max(at for at, b in out if b[0] == "attend0")
    second, latents_done1 = self0(max(attended + SELF0_AT[1], experts_done - scored), 1)
    out += first + second
    at = max(latents_done + CROSS1_AT[0], attended + 1.0)
    at1 = max(latents_done1 + CROSS1_AT[1], at + BATCH1[0] * BT)
    w_from, w_to = start0[6] + WEIGHTS1[0], at + WEIGHTS1[1]
    out += [(w_from + (w_to - w_from) * k / len(experts1), ("weight", *f)) for k, f in enumerate(experts1)]
    for b in range(BT):
        out += cross1(at + BATCH1[0] * b, b) + cross1(at1 + BATCH1[1] * b, BT + b)
    ends = [max(at for at, b in out if b[0] == "attend1" and b[1] == BT * t + BT - 1) + 0.7 for t in range(NT)]
    return out + linear1(ends[0], 0, EXPERT1) + linear1(ends[1], 1, EXPERT1_LAST)


PLAN = plan()


FIRST = [(("b1", 0), ("best1", 1)), (("y0", 0, NE0 - 1), ("best0", 1)), (("y0", 1, NE0 - 1), ("lin", 0)), (("y0", 1, NE0 - 1), ("hid1", 0, 0)),
         (("oT1", 0, 1), ("attend1", BT, C)), (("qk", 1, 3), ("oT1", 0, 0)), (("attend0", B - 1, C), ("qk", 0, 0)),
         (("weight", "w12T", E - 1), ("qk", 1, 0)), (("prep", B - 1, 2), ("xnT", 0)), (("attend0", B - 1, C - 1), ("lat1", 0))]

CHAIN = []
for tile_ in range(NT):
    steps_ = [("heads0", tile_), ("out0", tile_), ("ln", 1, tile_), ("xT", 1, tile_), ("dproj", tile_), ("dval", tile_),
              ("dsoft", tile_, 0), ("dsoft", tile_, 1), ("dprob", tile_, 0), ("dprob", tile_, 1), ("drms", tile_), ("doT", tile_), ("dout", tile_),
              ("ln", 2, tile_), ("xT", 2, tile_), ("gate0", tile_), ("best0", tile_)]
    steps_ += [("y0", tile_, i) for i in range(NE0)] + [("ln", 3, tile_), ("ln", 4, tile_), ("lat", tile_)]
    steps_ += [("out1", tile_), ("ln", 5, tile_), ("xT", 5, tile_), ("lin", tile_), ("linout", tile_), ("ln", 6, tile_), ("xT", 6, tile_),
               ("gate1", tile_), ("best1", tile_)] + [("y1", tile_, e) for e in range(E)] + [("b1", tile_)]
    CHAIN += list(zip(steps_, steps_[1:]))
CHAIN += [(("lam_end",), ("dprob", 0, 0)), (("rows",), ("heads0", 0)), (("weight", "g", 0), ("lin", 0))]


def order(part):
    blocks = [b for _, _, b in sorted((at + shift(b) + LAG.get(b[0], (0,) * 4)[part], i, b) for i, (at, b) in enumerate(PLAN))]
    place = {b: i for i, b in enumerate(blocks)}
    assert all(place[a] < place[b] for a, b in FIRST + (CHAIN if part == DVE else []))
    return blocks


ORDER = order(PE)
assert len(set(ORDER)) == len(ORDER)


def jobs_of(kind, *a):
    if kind == "start":
        return ["w0T", "b0T", ("xT", 0, 0), "q0T"]
    if kind == "rows":
        return ["rowsT", "bias0T", "w0oT"]
    if kind == "prep":
        return [(("ctxT", "k0T", "v0")[a[1]], a[0])]
    if kind == "attend0":
        return [("p0T", *a)] if a[1] < C else []
    if kind == "attend1":
        return [("p1T", *a)] if a[1] <= C else []
    if kind == "dproj":
        return [("qd", *a), ("kd", *a)]
    if kind == "dval":
        return [("vd", a[0], 0), ("vd", a[0], 1)]
    if kind == "lin":
        return [("ac", *a), ("z", *a)]
    if kind in ("weight", "out0", "xT", "doT", "dout", "gate0", "cwT0", "y0", "lat", "q1", "qk", "xnT", "lat1", "oT1", "daT",
                "out1", "linout", "gate1", "cwT1", "y1", "b1"):
        return [(kind, *a)]
    return []


def broadcast(ap, axis, n):
    ap = ap.unsqueeze(axis)
    shape = list(ap.shape)
    shape[axis] = n
    return ap.to_broadcast(shape)


def build(nc, d, out):
    with ExitStack() as ctx:
        def sb(name, shape, dt=F32):
            return ctx.enter_context(nc.sbuf_tensor(name, shape, dt))

        def sem(name):
            return ctx.enter_context(nc.semaphore(name))

        job, nth, kinds = {}, {}, {}
        for block_ in ORDER:
            kinds[block_[0]] = nth[block_] = kinds.get(block_[0], 0) + 1
            for key in jobs_of(*block_):
                job[key] = len(job)

        banks = ctx.enter_context(nc.psum_tensor("banks", [P, 8, 512], F32))
        acc = banks[:, 2, :]
        side = 3

        x_sb = sb("x_sb", [P, NT, D])
        xb_sb = sb("xb_sb", [P, NT, D])
        xln = sb("xln", [P, NT, D])
        lat = sb("lat", [P, NT, D])
        xT = sb("xT", [P, T])
        latT = sb("latT", [P, T])
        ctx_sb = sb("ctx_sb", [P, B, C, D])
        ctxT = sb("ctxT", [P, CT, S])
        k0T = sb("k0T", [P, KV, S])
        v0 = sb("v0", [P, KV, C, D])
        w11T = sb("w11T", [P, E, KH, P])
        w12T = sb("w12T", [P, E, KH, P])
        w13T = sb("w13T", [P, NE0, 4, P])
        w2T = sb("w2T", [P, NE0, D])
        w0T = sb("w0T", [P, 4, D])
        wraw1 = sb("wraw1", [P, RAW_SLOTS, KH, D])
        cols = sb("cols", [P, ROWS])
        bcol = sb("bcol", [P, 2, 2 * NE0])
        bc = sb("bc", [P, 6, D])
        gb = sb("gb", [P, E])
        alpha = sb("alpha", [P, 1])
        ws = sb("ws", [P, 3, 2 * D])
        wso = sb("wso", [P, 2, D])
        wq1 = sb("wq1", [P, 16 * HALF_H])
        wkv1 = sb("wkv1", [P, 32 * HALF_H])
        wout1 = sb("wout1", [P, 8, D])
        wkT = sb("wkT", [P, 8, D])
        lowr = sb("lowr", [P, 5, 32])
        uu = sb("uu", [P, 65])
        m12 = sb("m12", [P, P])
        woT = sb("woT", [P, D])
        gl = sb("gl", [65, D])
        b2x = sb("b2x", [NE0, D])
        b2y = sb("b2y", [E, D])
        negmask = sb("negmask", [P, B, S], BF16)

        ident = sb("ident", [P, P])
        sel16 = sb("sel16", [P, 16])
        sel4 = sb("sel4", [P, 4])
        mask4 = sb("mask4", [P, 4])
        mask4s = sb("mask4s", [P, 4])
        maskv = sb("maskv", [P, 16])
        caus3 = sb("caus3", [P, 4, Q])
        causal = sb("causal", [P, Q])
        iota8 = sb("iota8", [P, E])
        minus_half = sb("minus_half", [P, 16])
        icnt = sb("icnt", [64, BT, Q])
        keep = sb("keep", [64, BT, Q])

        qT = sb("qT", [P, T])
        qblk = sb("qblk", [P, B, HG, Q])
        big = sb("big", [P, 8, SL])
        pT = sb("pT", [P, C + 1, 512])
        stats = sb("stats", [P, 36, 6])
        mv = sb("mv", [P, 36, 2])
        rstd = sb("rstd", [P, 36])
        nmr = sb("nmr", [P, 36])
        nlat = sb("nlat", [P, 2, G])
        nmax = sb("nmax", [P, 2 * B * G])
        rsum = sb("rsum", [P, 2 * B * G])
        rinv = sb("rinv", [P, 2 * B * G])
        oT = sb("oT", [P, 8, P])
        small = sb("small", [P, 12, 16])
        lam = sb("lam", [P, 3, 16])
        m8 = sb("m8", [P, 8])
        ix = sb("ix", [P, 8], U32)
        cw = sb("cw", [P, NE0])
        cwT = sb("cwT", [NE0, P])
        vblk = sb("vblk", [P, BT, 16, 16])
        kblk = sb("kblk", [P, 2 * BT, HG, Q])
        qdT = sb("qdT", [P, 2, P])
        sc = sb("sc", [P, G, 2 * BT * Q])
        hid = sb("hid", [P, 2, KH, P])
        tmp = sb("tmp", [P, 2, 3, P])

        def flat(t):
            names = "abcde"[:len(t.shape) - 1]
            return t[:].rearrange(f"p {' '.join(names)} -> p ({' '.join(names)})") if len(names) > 1 else t[:]

        def view(t, first, *shape, parts=P):
            v = flat(t)[0:parts, first:first + int(np.prod(shape))]
            names = "abcde"[:len(shape)]
            sizes = dict(zip(names, shape))
            return v.rearrange(f"p ({' '.join(names)}) -> p {' '.join(names)}", **sizes) if len(names) > 1 else v

        w1raw0 = view(w11T, 0, 2, 2 * E, D)
        w2raw = view(w12T, 0, NE0, P)
        w0raw = view(w12T, 9 * D, 4, D)
        shared_raw = view(w12T, 13 * D, 4, D)
        wl = view(w12T, 17 * D, 3, D)
        rows = view(w12T, 20 * D, D, parts=ROWS)
        brow = view(w12T, 21 * D, 2 * P, parts=2 * NE0)
        mask_u8 = w12T[:].bitcast(U8).rearrange("p e k m -> p (e k m)")[:, 23 * D * 4:23 * D * 4 + B * S].rearrange("p (b s) -> p b s", b=B)
        qk = [view(r, 0, BT, 16, Q) for r in (k0T, wraw1)]
        yT = view(v0, 0, 16, P)
        xnT = ctxT
        x_rep = view(sc, 0, BT, 4, Q)
        attn = view(kblk, 0, 4, P)
        attnT = view(kblk, 4 * P, 4, P)
        own = view(kblk, 0, 4 * P)
        on = view(vblk, 0, 2, P)
        o0T = view(kblk, 4 * P, P)
        q1T = oT
        odT = qdT
        lam_in = view(hid, 0, 4, 16, 8)
        scan = view(tmp, 0, 3, P, parts=65)
        scan_c = view(kblk, 0, P, parts=64)

        x_loaded = sem("x_loaded")
        w0_loaded = sem("w0_loaded")
        b0_loaded = sem("b0_loaded")
        rows_loaded = sem("rows_loaded")
        ctx_loaded = [sem(f"ctx_loaded{b}") for b in range(B)]
        bc_loaded = sem("bc_loaded")
        mask_loaded = sem("mask_loaded")
        self_loaded = sem("self_loaded")
        exp0_loaded = [sem(f"exp0_loaded{h}") for h in range(2)]
        exp0_w2_loaded = sem("exp0_w2_loaded")
        b2_loaded = sem("b2_loaded")
        wkv_loaded = sem("wkv_loaded")
        wq1_loaded = sem("wq1_loaded")
        lin_loaded = sem("lin_loaded")
        exp1_loaded = [sem(f"exp1_loaded{s}") for s in range(RAW_SLOTS)]
        out_stored = sem("out_stored")
        pool_step = sem("pool_step")
        dve_step = sem("dve_step")
        act_step = sem("act_step")
        ring_filled = [sem(f"ring_filled{i}") for i in range(RING)]
        ring_copied = [sem(f"ring_copied{i}") for i in range(RING)]
        ident_ready = sem("ident_ready")
        consts_ready = sem("consts_ready")
        negmask_ready = sem("negmask_ready")
        bias_added = sem("bias_added")
        ln_var = sem("ln_var")
        ln_rstd = sem("ln_rstd")
        ln_done = sem("ln_done")
        cstat_ready = sem("cstat_ready")
        xn_ready = sem("xn_ready")
        qblk_ready = sem("qblk_ready")
        s_filled = sem("s_filled")
        s_max = sem("s_max")
        s_exp = sem("s_exp")
        s_rinv = sem("s_rinv")
        p_ready = sem("p_ready")
        av_read = sem("av_read")
        acc_read = sem("acc_read")
        o0T_ready = sem("o0T_ready")
        d_filled = sem("d_filled")
        d_sub = sem("d_sub")
        d_exp = sem("d_exp")
        d_attn = sem("d_attn")
        d_out = sem("d_out")
        d_sq = sem("d_sq")
        d_ms = sem("d_ms")
        d_rms = sem("d_rms")
        d_on = sem("d_on")
        wso_ready = sem("wso_ready")
        lam_sum = sem("lam_sum")
        lam_exp = sem("lam_exp")
        uu_ready = sem("uu_ready")
        g_max = sem("g_max")
        cw_ready = sem("cw_ready")
        h_filled = sem("h_filled")
        h_act = sem("h_act")
        h_prod = sem("h_prod")
        g_ready = sem("g_ready")
        tanh_ready = sem("tanh_ready")
        l_ready = sem("l_ready")
        a_ready = sem("a_ready")
        h1_filled = sem("h1_filled")
        h1_even = sem("h1_even")
        h1_odd = sem("h1_odd")
        pr_ready = sem("pr_ready")

        block = ctx.enter_context(nc.Block())

        def bank(key):
            return banks[:, 5 + job[key] % RING, :]

        def wait_bank_free(pe, key):
            if job[key] >= RING:
                pe.wait_ge(ring_copied[job[key] % RING], job[key] // RING)

        def wait_filled(eng, key):
            eng.wait_ge(ring_filled[job[key] % RING], job[key] // RING + 1)

        def wait_copied(eng, key):
            eng.wait_ge(ring_copied[job[key] % RING], job[key] // RING + 1)

        def filled(ins, key):
            ins.then_inc(ring_filled[job[key] % RING], 1)

        def copied(ins, key):
            ins.then_inc(ring_copied[job[key] % RING], 1)

        def tile0(b, g):
            return G * b + g

        def tile1(b, g):
            return G * (B + b) + g

        def chunks_read(layer, b, c):
            return C * b + c + 1 if layer == 0 else C * B + (C + 1) * b + c + 1

        @block.sync
        def _(sp):
            def load(dst, src, loaded):
                sp.dma_start(dst, src).then_inc(loaded, 16)

            def load_ctx(b):
                load(ctx_sb[:, b, :, :], d["ctx_1024"][b].rearrange("(p c) d -> p c d", c=C), ctx_loaded[b])

            load(x_sb[:], d["x"].rearrange("b q d -> (b q) d").rearrange("(t p) d -> p t d", p=P), x_loaded)
            for i, n in enumerate(("Wq", "Wk", "Wv")):
                load(w0raw[:, i, :], d["L0_xattn_" + n], w0_loaded)
            for i, n in enumerate(("L0_xattn_bq", "L0_xattn_bk", "L0_xattn_bv")):
                load(rows[i:i + 1, :], d[n].rearrange("(o n) -> o n", o=1), b0_loaded)
            load_ctx(0)
            load_ctx(1)
            load(w0raw[:, 3, :], d["L0_xattn_Wo"], rows_loaded)
            for i, n in enumerate(("L1_attn_bias_b", "L1_attn_bias_t")):
                load(rows[3 + i:4 + i, :], d[n].rearrange("(o n) -> o n", o=1), rows_loaded)
            load(rows[5:6, :].rearrange("o (h d) -> o h d", d=16),
                 broadcast(d["L0_attn_rms_scale"].rearrange("(o n) -> o n", o=1), 1, 8), rows_loaded)
            load(rows[6:14, :], d["L0_ffn_gate_w"], rows_loaded)
            load(rows[14:22, :], d["L1_ffn_gate_w"], rows_loaded)
            load(rows[22:54, :], d["L1_ffn_b1"].rearrange("e (k p) -> (e k) p", p=P), rows_loaded)
            load(brow[0:E, :], d["L0_ffn_b1"], rows_loaded)
            load(brow[E:E + 1, :], d["L0_ffn_sb1"].rearrange("(o n) -> o n", o=1), rows_loaded)
            load(brow[NE0:NE0 + E, :], d["L0_ffn_b3"], rows_loaded)
            load(brow[NE0 + E:, :], d["L0_ffn_sb3"].rearrange("(o n) -> o n", o=1), rows_loaded)
            load_ctx(2)
            for i, n in enumerate(("L0_xattn_bo", "L1_xattn_bout", "L1_xattn_g_media", "L1_xattn_b_media",
                                   "L1_xattn_g_latent", "L1_xattn_b_latent")):
                load(bc[:, i, :], d[n].partition_broadcast(P), bc_loaded)
            load(gb[:], d["L0_ffn_gate_b"].partition_broadcast(P), bc_loaded)
            load(alpha[:], d["L1_attn_alpha"].partition_broadcast(P), bc_loaded)
            load(w2raw[:, 0:E, :], d["L0_ffn_w2"].rearrange("e d f -> d e f"), exp0_w2_loaded)
            load(w2raw[:, E, :], d["L0_ffn_sw2"], exp0_w2_loaded)
            load_ctx(3)
            for h in range(2):
                es = slice(4 * h, 4 * h + 4)
                for w, n in enumerate(("L0_ffn_w1", "L0_ffn_w3")):
                    load(w1raw0[:, w, 8 * h:8 * h + 8, :].rearrange("p (e r) d -> p e r d", r=2),
                         d[n][es].rearrange("e (i r) d -> i e r d", r=2), exp0_loaded[h])
                if h == 0:
                    for w, n in enumerate(("L0_ffn_sw1", "L0_ffn_sw3")):
                        load(shared_raw[:, 2 * w:2 * w + 2, :], d[n].rearrange("(i r) d -> i r d", r=2), exp0_loaded[0])
                load_ctx(4 + h)
            for i, n in enumerate(("Wq", "Wk", "Wv")):
                load(ws[:, i, :], d["L0_attn_" + n], self_loaded)
            load(wso[:], d["L0_attn_Wo"].rearrange("(t p) d -> p t d", p=P), self_loaded)
            for i, n in enumerate(("q1", "k1", "q2", "k2")):
                load(lam_in[:, i, :, :], d["L0_attn_lambda_" + n].partition_broadcast(P), self_loaded)
            for i, n in enumerate(("Wq", "Wk", "Wo")):
                load(wl[:, i, :], d["L1_attn_" + n], lin_loaded)
            for i, n in enumerate(("V_b", "V_t", "W_b", "W_t", "X_t")):
                load(lowr[:, i, :], d["L1_attn_" + n], lin_loaded)
            load(uu[:, 0:32], d["L1_attn_U_b"], lin_loaded)
            load(uu[:, 32:64], d["L1_attn_U_t"], lin_loaded)
            load_ctx(6)
            load_ctx(7)
            load(mask_u8, d["mask_BxS2_bk0"].partition_broadcast(P), mask_loaded)
            load(b2x[0:E, :], d["L0_ffn_b2"], b2_loaded)
            load(b2x[E:, :], d["L0_ffn_sb2"].rearrange("(o n) -> o n", o=1), b2_loaded)
            load(b2y[:], d["L1_ffn_b2"], b2_loaded)
            load(wkv1[:], d["L1_xattn_Wkv"], wkv_loaded)
            load(wq1[:], d["L1_xattn_Wq"], wq1_loaded)
            load(wout1[:], d["L1_xattn_Wout"].rearrange("(i p) n -> p i n", p=P), wq1_loaded)
            raw = [("w11T", e) for e in range(E)] + [("w12T", e) for e in range(E)]
            for i, (what, e) in enumerate(raw):
                if i >= RAW_SLOTS:
                    wait_filled(sp, ("weight", *raw[i - RAW_SLOTS]))
                slot = wraw1[:, i % RAW_SLOTS]
                if what == "w11T":
                    load(slot, d["L1_ffn_w1"][e].rearrange("(k p) d -> p k d", p=P), exp1_loaded[i % RAW_SLOTS])
                else:
                    load(slot.rearrange("p k d -> p (k d)"), d["L1_ffn_w2"][e], exp1_loaded[i % RAW_SLOTS])
            rows_out = out.rearrange("b q d -> (b q) d")
            for kind, *a in ORDER:
                if kind == "store":
                    wait_copied(sp, ("b1", *a))
                    sp.dma_start(rows_out[P * a[0]:P * a[0] + P, :], x_sb[:, a[0], :]).then_inc(out_stored, 16)
            sp.wait_ge(out_stored, 16 * NT)

        @block.gpsimd
        def _(pool):
            n = 0

            def step(ins):
                nonlocal n
                n += 1
                ins.then_inc(pool_step, 1)
                pool.wait_ge(pool_step, n)

            def inv_sqrt(dst, src):
                return nc.gpsimd.tensor_tensor(dst, src, minus_half[:, 0:src.shape[1]], ALU.pow)

            def select(ap, base, c, *pattern):
                step(nc.gpsimd.affine_select(out=ap, in_=ap, compare_op=ALU.is_ge, fill=0.0, base=base,
                                             pattern=list(pattern), channel_multiplier=c))

            def start():
                step(nc.gpsimd.memset(ident[:], 0.0))
                nc.gpsimd.affine_select(out=ident[:], in_=ident[:], compare_op=ALU.not_equal, fill=1.0, base=0,
                                        pattern=[[-1, P]], channel_multiplier=1).then_inc(ident_ready, 1)
                step(nc.gpsimd.memset(minus_half[:], -0.5))
                pool.wait_ge(ln_var, 1)
                inv_sqrt(rstd[:, 32:34], rstd[:, 32:34]).then_inc(ln_rstd, 1)
                nc.gpsimd.memset(sel16[:], 1.0)
                nc.gpsimd.memset(sel4[:], 1.0)
                nc.gpsimd.memset(keep[:], 1.0)
                nc.gpsimd.memset(cw[:], 1.0)
                step(nc.gpsimd.memset(caus3[:], NEG))
                select(sel16[:], 0, 1, [-8, 16])
                select(sel16[:], 7, -1, [8, 16])
                select(sel4[:], 0, 1, [-Q, 4])
                select(sel4[:], Q - 1, -1, [Q, 4])
                select(caus3[:], 0, 1, [-Q, 4], [0, Q])
                select(caus3[:], Q - 1, -1, [Q, 4], [0, Q])
                select(caus3[:], -1, -1, [Q, 4], [1, Q])
                nc.gpsimd.iota(iota8[:], pattern=[[1, E]], base=0, channel_multiplier=0, allow_small_or_imprecise_dtypes=True)
                nc.gpsimd.iota(icnt[:], pattern=[[0, BT], [1, Q]], base=1, channel_multiplier=0, allow_small_or_imprecise_dtypes=True)
                nc.gpsimd.memset(keep[:, :, 0:1], 0.0).then_inc(consts_ready, 1)
                pool.wait_ge(bc_loaded, 16 * 8)
                pool.wait_ge(x_loaded, 16)
                nc.gpsimd.tensor_tensor(xb_sb[:], x_sb[:], broadcast(bc[:, 0, :], 1, NT), ALU.add).then_inc(bias_added, 1)

            def ln(k, t):
                pool.wait_ge(ln_var, 1 + nth[("ln", k, t)])
                inv_sqrt(rstd[:, 34 + t:35 + t], rstd[:, 34 + t:35 + t]).then_inc(ln_rstd, 1)

            def cnorm(b, k):
                cs = slice(C * b, C * b + C)
                if k == 0:
                    pool.wait_ge(cstat_ready, b + 1)
                    step(inv_sqrt(rstd[:, cs], rstd[:, cs]))
                    step(nc.gpsimd.tensor_tensor(nmr[:, cs], nmr[:, cs], rstd[:, cs], ALU.mult))
                    wait_filled(pool, ("ctxT", b))
                    for c in range(C):
                        i = C * b + c
                        ins = nc.gpsimd.tensor_scalar(ctx_sb[:, b, c, :], ctx_sb[:, b, c, :], rstd[:, i:i + 1], nmr[:, i:i + 1],
                                                      ALU.mult, ALU.add)
                    step(ins)
                if k == 1:
                    step(nc.gpsimd.tensor_tensor(ctx_sb[:, b], ctx_sb[:, b], broadcast(bc[:, 2, :], 1, C), ALU.mult))
                if k == 2:
                    nc.gpsimd.tensor_tensor(ctx_sb[:, b], ctx_sb[:, b], broadcast(bc[:, 3, :], 1, C), ALU.add).then_inc(xn_ready, 1)

            def mask(n):
                pool.wait_ge(mask_loaded, 16)
                for b in (2 * n, 2 * n + 1):
                    ins = nc.gpsimd.tensor_scalar(negmask[:, b, :].rearrange("q (c p) -> q c p", p=P),
                                                  mask_u8[:, b, :].rearrange("q (p c) -> q c p", c=C), NEG, 1.0, ALU.mult, ALU.mult)
                ins.then_inc(negmask_ready, 1)

            def normalise(first, b, width):
                pool.wait_ge(s_rinv, first // G + 1)
                for g in range(G):
                    t = big[:, (b % 2) * G + g, 0:width]
                    nc.gpsimd.tensor_scalar(t, t, rinv[:, first + g:first + g + 1], 1.0, ALU.mult, ALU.mult).then_inc(p_ready, 1)


            def drms(t):
                pool.wait_ge(d_ms, nth[("drms", t)])
                inv_sqrt(small[:, 0, :], small[:, 0, :]).then_inc(d_rms, 1)

            def hid0(t, i):
                k = nth[("hid0", t, i)]
                pool.wait_ge(h_prod, k)
                nc.gpsimd.tensor_scalar(tmp[:, k % 2, 1, :], tmp[:, k % 2, 1, :], 7.0, -7.0, ALU.min, ALU.max).then_inc(l_ready, 1)

            def lat_(t):
                wait_copied(pool, ("y0", t, NE0 - 1))
                nc.gpsimd.tensor_tensor(xb_sb[:, t, :], x_sb[:, t, :], bc[:, 1, :], ALU.add).then_inc(bias_added, 1)

            parts = {"start": start, "ln": ln, "cnorm": cnorm, "mask": mask, "norm0": lambda b: normalise(tile0(b, 0), b, S),
                     "norm1": lambda b: normalise(tile1(b, 0), b, SL), "drms": drms, "hid0": hid0, "lat": lat_}
            for kind, *a in order(POOL):
                if kind in parts:
                    parts[kind](*a)

        @block.scalar
        def _(act):
            n = 0

            def step(ins):
                nonlocal n
                n += 1
                ins.then_inc(act_step, 1)
                act.wait_ge(act_step, n)

            def copy_job(key, dst, src):
                wait_filled(act, key)
                copied(nc.scalar.activation(dst, src, ACT.Copy), key)

            def start():
                copy_job("w0T", w0T[:, 0:3, :].rearrange("p i d -> p (i d)"), bank("w0T")[:, 0:3 * D])
                copy_job("b0T", cols[:, 0:3], bank("b0T")[:, 0:3])
                copy_job(("xT", 0, 0), xT[:], bank(("xT", 0, 0))[:, 0:T])
                wait_filled(act, "q0T")
                wait_copied(act, "b0T")
                copied(nc.scalar.activation(qT[:], bank("q0T")[:, 0:T], ACT.Identity, bias=cols[:, 0:1]), "q0T")

            def rows_():
                copy_job("rowsT", cols[:, 3:], bank("rowsT")[:, 3:ROWS])
                copy_job("bias0T", bcol[:].rearrange("p r i -> p (r i)"), bank("bias0T")[:, 0:4 * NE0])
                copy_job("w0oT", w0T[:, 3, :], bank("w0oT")[:, 0:D])

            def prep(b, k):
                if k == 0:
                    if b >= CT:
                        wait_filled(act, ("v0", b - CT))
                    copy_job(("ctxT", b), ctxT[:, b % CT, :], bank(("ctxT", b)))
                if k == 1:
                    if b >= KV:
                        act.wait_ge(s_filled, tile0(b - KV, G - 1) + 1)
                    wait_filled(act, ("k0T", b))
                    copied(nc.scalar.activation(k0T[:, b % KV, :], bank(("k0T", b)), ACT.Identity, bias=cols[:, 1:2]), ("k0T", b))

            def weight(what, e):
                key = ("weight", what, e)
                if what == "w13T" and e % 2:
                    copy_job(key, w13T[:, e].rearrange("p f i -> p (f i)"), bank(key))
                if what == "wkT":
                    copy_job(key, wkT[:, 4 * e:4 * e + 4, :].rearrange("p i d -> p (i d)"), bank(key))
                if what == "w11T":
                    if e == 0:
                        wait_filled(act, ("weight", "w13T", E - 1))
                    copy_job(key, w11T[:, e].rearrange("p k m -> p (k m)"), bank(key))
                if what == "w12T":
                    if e == 0:
                        wait_filled(act, ("weight", "m12", 0))
                        wait_filled(act, ("weight", "woT", 0))
                        wait_filled(act, ("weight", "w13T", E))
                        act.wait_ge(negmask_ready, BT)
                    copy_job(key, w12T[:, e].rearrange("p k m -> p (k m)"), bank(key))

            def exp_tile(k, dst, src, scale):
                act.wait_ge(s_max, k + 1)
                nc.scalar.activation(dst, src, ACT.Exp, bias=nmax[:, k:k + 1], scale=scale,
                                     accum_out=rsum[:, k:k + 1]).then_inc(s_exp, 1)

            def scores0(b, g):
                if b >= 2:
                    wait_filled(act, ("p0T", b - 2, C - 1))
                exp_tile(tile0(b, g), big[:, (b % 2) * G + g, 0:S], banks[:, g % 2, :], 1.0)

            def scores1(b, g):
                t = big[:, (b % 2) * G + g, :]
                exp_tile(tile1(b, g), t, t, -1.0)

            def attend0(b, c):
                if c < C and c not in DVE_CHUNKS[0][b // BT]:
                    if b:
                        act.wait_ge(av_read, chunks_read(0, b - 1, c))
                    copy_job(("p0T", b, c), pT[:, c, :], bank(("p0T", b, c)))

            def attend1(b, c):
                key = ("p1T", b, c)
                if c <= C and c not in DVE_CHUNKS[1][b // BT] and b:
                    act.wait_ge(av_read, chunks_read(1, b - 1, c))
                if c < C and c not in DVE_CHUNKS[1][b // BT]:
                    copy_job(key, pT[:, c, :], bank(key))
                if c == C:
                    r = Q * (b % BT)
                    copy_job(key, pT[r:r + Q, c, :], bank(key)[0:Q, :])

            def xT_(k, t):
                key = ("xT", k, t)
                src = bank(key)[:, 0:P]
                if k != 1:
                    copy_job(key, xT[:, P * t:P * t + P], src)
                    return
                wait_filled(act, key)
                step(nc.scalar.activation(xT[:, P * t:P * t + P], src, ACT.Copy))
                copied(nc.scalar.activation(x_rep, broadcast(src.rearrange("p (b q) -> p b q", q=Q), 2, 4), ACT.Copy), key)

            def lam_dots():
                act.wait_ge(lam_sum, 1)
                nc.scalar.activation(lam[:, 0:2, :], lam[:, 0:2, :], ACT.Exp).then_inc(lam_exp, 1)

            def dproj(t):
                copy_job(("qd", t), qdT[:].rearrange("p r t -> p (r t)"), bank(("qd", t))[:, 0:2 * P])

            def dsoft(t, p):
                act.wait_ge(d_sub, nth[("dsoft", t, p)])
                s2 = sc[:, 2 * p:2 * p + 2, :]
                nc.scalar.activation(s2, s2, ACT.Exp).then_inc(d_exp, 1)

            def dpv(t):
                act.wait_ge(d_out, t + 1)
                nc.scalar.activation(view(sc, 0, 2 * P), banks[:, side, 0:2 * P], ACT.Square).then_inc(d_sq, 1)

            def doT(t):
                copy_job(("doT", t), odT[:].rearrange("p f t -> p (f t)"), bank(("doT", t))[:, 0:2 * P])

            def gate(key):
                act.wait_ge(g_max, gate_nth[key])
                copied(nc.scalar.activation(small[:, 1, 0:E], bank(key)[:, 0:E], ACT.Exp, bias=small[:, 2, 0:1],
                                            accum_out=small[:, 2, 1:2]), key)

            def cwT_(layer, t):
                copy_job((f"cwT{layer}", t), cwT[:], bank((f"cwT{layer}", t))[0:NE0, 0:P])

            def hid0(t, i):
                k, e = nth[("hid0", t, i)], (i + E) % NE0
                act.wait_ge(h_filled, k)
                if k > 2:
                    act.wait_ge(h_prod, k - 2)
                h1 = banks[:, side + k % 2, 0:2 * P].rearrange("p (r t) -> p r t", r=2)
                for r in range(2):
                    ins = nc.scalar.activation(hid[:, k % 2, r, :], h1[:, r, :], ACT.Identity, bias=bcol[:, r, e:e + 1])
                ins.then_inc(h_act, 1)

            def act0(t, i):
                k = nth[("act0", t, i)]
                act.wait_ge(g_ready, k)
                if k > 2:
                    act.wait_ge(a_ready, k - 2)
                nc.scalar.activation(hid[:, k % 2, 2, :], tmp[:, k % 2, 0, :], ACT.Tanh, scale=1.702 / 2).then_inc(tanh_ready, 1)

            def lat_(t):
                copy_job(("lat", t), latT[:, P * t:P * t + P], bank(("lat", t))[:, 0:P])

            def q1(t, n):
                key = ("q1", t, n)
                wait_filled(act, key)
                copied(nc.scalar.activation(q1T[:, 4 * n:4 * n + 4, :].rearrange("p i t -> p (i t)"), bank(key), ACT.Copy,
                                            scale=HALF_H ** -0.5), key)

            def qk_(t, n):
                if n % 2 == 0:
                    copy_job(("qk", t, n), qk[t][:, :, n // 2 * 8 + n % 2:n // 2 * 8 + 8:2, :].rearrange("p b h q -> p h b q"),
                             bank(("qk", t, n)).rearrange("p (h b q) -> p h b q", h=4, b=BT))

            def xnT_(b):
                if b >= CT:
                    act.wait_ge(s_filled, tile1(b - CT, G - 1) + 1)
                copy_job(("xnT", b), xnT[:, b % CT, :], bank(("xnT", b)))

            def oT1(t, n):
                if n == 0:
                    copy_job(("oT1", t, n), oT[:, 4 * n:4 * n + 4, :].rearrange("p i t -> p (i t)"), bank(("oT1", t, n)))

            def hid1(t, e):
                if e % 2:
                    return
                act.wait_ge(h1_filled, nth[("hid1", t, e)])
                if e >= 2:
                    wait_filled(act, ("y1", t, e - 2))
                elif t:
                    wait_filled(act, ("y1", t - 1, E - 2 + e))
                for k in range(KH):
                    ins = nc.scalar.activation(hid[:, e % 2, k, :], banks[:, side + e % 2, P * k:P * k + P], ACT.Relu,
                                               bias=cols[:, 22 + KH * e + k:23 + KH * e + k])
                ins.then_inc(h1_even, 1)

            parts = {"start": start, "rows": rows_, "prep": prep, "weight": weight, "scores0": scores0, "scores1": scores1, "attend0": attend0,
                     "lam_dots": lam_dots, "attend1": attend1, "xT": xT_, "dproj": dproj, "dsoft": dsoft,
                     "daT": lambda t: copy_job(("daT", t), attnT.rearrange("p g t -> p (g t)"), bank(("daT", t))), "dpv": dpv, "doT": doT,
                     "gate0": lambda t: gate(("gate0", t)), "gate1": lambda t: gate(("gate1", t)),
                     "cwT0": lambda t: cwT_(0, t), "cwT1": lambda t: cwT_(1, t), "hid0": hid0, "act0": act0, "lat": lat_, "q1": q1,
                     "qk": qk_, "xnT": xnT_, "oT1": oT1, "hid1": hid1}
            gate_nth = {key: i + 1 for i, key in enumerate(k for k in ORDER if k[0] in ("gate0", "gate1"))}
            for kind, *a in order(ACTE):
                if kind in parts:
                    parts[kind](*a)

        @block.vector
        def _(dve):
            n = 0

            def step(ins):
                nonlocal n
                n += 1
                ins.then_inc(dve_step, 1)
                dve.wait_ge(dve_step, n)

            def copy_job(key, dst, src):
                wait_filled(dve, key)
                copied(nc.vector.tensor_copy(dst, src), key)

            def variance(srcs, at):
                for i, src in enumerate(srcs):
                    ins = nc.vector.bn_stats(stats[:, at + i, :], src)
                step(ins)
                for i in range(len(srcs)):
                    ins = nc.vector.bn_aggr(mv[:, at + i, :], stats[:, at + i, :])
                step(ins)
                return nc.vector.tensor_scalar(rstd[:, at:at + len(srcs)], mv[:, at:at + len(srcs), 1], LN_EPS, None, ALU.add)

            def normalised(dst, src, at):
                return nc.vector.tensor_scalar(dst, src, mv[:, at, 0:1], rstd[:, at:at + 1], ALU.subtract, ALU.mult)

            def make_qblk(dst, src, count):
                return nc.vector.tensor_tensor(dst, broadcast(src.rearrange("p (b q) -> p b q", q=Q), 2, HG),
                                               broadcast(broadcast(mask4s[:], 1, count), 3, Q), ALU.mult)

            def start():
                dve.wait_ge(x_loaded, 16)
                variance([x_sb[:, t, :] for t in range(NT)], 32).then_inc(ln_var, 1)
                dve.wait_ge(ln_rstd, 1)
                normalised(xln[:, 0, :], x_sb[:, 0, :], 32)
                normalised(xln[:, 1, :], x_sb[:, 1, :], 33).then_inc(ln_done, 1)
                dve.wait_ge(consts_ready, 1)
                step(nc.vector.tensor_reduce(mask4[:], sel16[:].rearrange("p (g j) -> p j g", j=4), AX, ALU.add))
                nc.vector.tensor_scalar(mask4s[:], mask4[:], float(8.0 ** -0.5), None, ALU.mult)
                nc.vector.tensor_copy(maskv[:].rearrange("p (m g h) -> p m g h", g=G, h=2),
                                      broadcast(sel4[:].rearrange("p (m h) -> p m h", h=2), 2, G))
                nc.vector.tensor_reduce(causal[:], caus3[:].rearrange("p j k -> p k j"), AX, ALU.add)
                step(nc.vector.reciprocal(icnt[:], icnt[:]))
                wait_copied(dve, "q0T")
                make_qblk(qblk[:], qT[:], B).then_inc(qblk_ready, 1)

            def prep(b, k):
                if k == 2:
                    if b >= KV:
                        dve.wait_ge(av_read, chunks_read(0, b - KV, C - 1))
                    copy_job(("v0", b), v0[:, b % KV].rearrange("p c d -> p (c d)"), bank(("v0", b)))

            def cstat(b):
                dve.wait_ge(ctx_loaded[b], 16)
                cs = slice(C * b, C * b + C)
                variance([ctx_sb[:, b, c, :] for c in range(C)], C * b)
                nc.vector.tensor_scalar(nmr[:, cs], mv[:, cs, 0], -1.0, None, ALU.mult).then_inc(cstat_ready, 1)

            def weight(what, e):
                key = ("weight", what, e)
                if what == "w13T" and e % 2 == 0:
                    copy_job(key, w13T[:, e].rearrange("p f i -> p (f i)"), bank(key))
                if what == "w2T":
                    m = min(4, NE0 - 4 * e)
                    wait_filled(dve, key)
                    copied(nc.vector.tensor_scalar(w2T[:, 4 * e:4 * e + m, :].rearrange("p e d -> p (e d)"), bank(key)[:, 0:P * m],
                                                   0.5, None, ALU.mult), key)
                if what == "m12":
                    copy_job(key, m12[:], bank(key)[:, 0:P])
                    dve.wait_ge(lin_loaded, 16 * 10)
                    dve.wait_ge(bc_loaded, 16 * 8)
                    wait_copied(dve, "rowsT")
                    nc.vector.scalar_tensor_tensor(uu[:, 64:65], cols[:, 4:5], alpha[:, 0:1], cols[:, 3:4], ALU.mult, ALU.add)
                    nc.vector.tensor_scalar(uu[:, 32:64], uu[:, 32:64], alpha[:, 0:1], None, ALU.mult).then_inc(uu_ready, 1)
                if what == "woT":
                    copy_job(key, woT[:], bank(key)[:, 0:P])
                if what == "g":
                    copy_job(key, gl[:], bank(key)[0:65, 0:P])

            def invert_sums(k):
                dve.wait_ge(s_exp, k + G)
                nc.vector.reciprocal(rinv[:, k:k + G], rsum[:, k:k + G]).then_inc(s_rinv, 1)

            def scores0(b, g):
                k = tile0(b, g)
                dve.wait_ge(s_filled, k + 1)
                nc.vector.tensor_reduce(nmax[:, k:k + 1], banks[:, g % 2, :], AX, ALU.max, negate=True).then_inc(s_max, 1)

            def lat1(b):
                key = ("lat1", b)
                wait_filled(dve, key)
                if b >= 2:
                    wait_filled(dve, ("p1T", b - 2, C))
                s4 = bank(key)[:, 0:G * Q].rearrange("p (g k) -> p g k", g=G)
                nc.vector.tensor_reduce(nlat[:, b % 2, :], s4, AX, ALU.max, negate=True)
                copied(nc.vector.tensor_scalar(big[:, (b % 2) * G:(b % 2) * G + G, S:], s4, -1.0, None, ALU.mult), key)
                wait_copied(dve, key)

            def scores1(b, g):
                k = tile1(b, g)
                if k == tile1(0, 0):
                    dve.wait_ge(negmask_ready, BT)
                dve.wait_ge(s_filled, k + 1)
                nc.vector.tensor_tensor_reduce(out=big[:, (b % 2) * G + g, 0:S], in0=banks[:, g % 2, :], in1=negmask[:, b, :],
                                               scale=-1.0, scalar=nlat[:, b % 2, g:g + 1], op0=ALU.add, op1=ALU.min,
                                               accum_out=nmax[:, k:k + 1]).then_inc(s_max, 1)

            def attend0(b, c):
                if c in DVE_CHUNKS[0][b // BT]:
                    if b:
                        dve.wait_ge(av_read, chunks_read(0, b - 1, c))
                    copy_job(("p0T", b, c), pT[:, c, :], bank(("p0T", b, c)))

            def attend1(b, c):
                if c in DVE_CHUNKS[1][b // BT]:
                    if b:
                        dve.wait_ge(av_read, chunks_read(1, b - 1, c))
                    copy_job(("p1T", b, c), pT[:, c, :], bank(("p1T", b, c)))
                if c == C + 1:
                    dve.wait_ge(av_read, chunks_read(1, b, C))
                    nc.vector.tensor_copy(yT[:, :, Q * (b % BT):Q * (b % BT) + Q], acc.rearrange("p (h q) -> p h q", q=Q)).then_inc(acc_read, 1)

            def add_to_x(key, t, base):
                wait_filled(dve, key)
                copied(nc.vector.tensor_tensor(x_sb[:, t, :], bank(key)[:, 0:P], base, ALU.add), key)
                wait_copied(dve, key)

            def heads0(t):
                dve.wait_ge(av_read, chunks_read(0, BT * t + BT - 1, C - 1))
                step(nc.vector.tensor_tensor(own.rearrange("p (b q j) -> p b j q", b=BT, j=HG),
                                             acc.rearrange("p (b j q) -> p b j q", b=BT, j=HG),
                                             broadcast(broadcast(mask4[:], 1, BT), 3, Q), ALU.mult))
                step(nc.vector.tensor_reduce(o0T, own.rearrange("p (t j) -> p t j", j=HG), AX, ALU.add))
                nc.vector.tensor_scalar(o0T, o0T, cols[:, 2:3], None, ALU.add).then_inc(o0T_ready, 1)

            def out0(t):
                dve.wait_ge(bias_added, 1)
                add_to_x(("out0", t), t, xb_sb[:, t, :])

            def ln(k, t):
                src = x_sb[:, t, :] if k != 4 else xln[:, t, :]
                if k == 4:
                    dve.wait_ge(ln_rstd, 1 + nth[("ln", 3, t)])
                    step(normalised(xln[:, t, :], x_sb[:, t, :], 34 + t))
                variance([src], 34 + t).then_inc(ln_var, 1)

            def xT_(k, t):
                dve.wait_ge(ln_rstd, 1 + nth[("ln", k, t)])
                normalised(xln[:, t, :], x_sb[:, t, :], 34 + t).then_inc(ln_done, 1)

            def lam_dots():
                dve.wait_ge(self_loaded, 16 * 8)
                v = lam_in[:].rearrange("p i h d -> p i (h d)")
                nc.vector.tensor_tensor(v[:, 0, :], v[:, 0, :], v[:, 1, :], ALU.mult)
                step(nc.vector.tensor_tensor(v[:, 2, :], v[:, 2, :], v[:, 3, :], ALU.mult))
                nc.vector.tensor_reduce(lam[:, 0, :], lam_in[:, 0], AX, ALU.add)
                nc.vector.tensor_reduce(lam[:, 1, :], lam_in[:, 2], AX, ALU.add).then_inc(lam_sum, 1)

            def lam_end():
                dve.wait_ge(lam_exp, 1)
                step(nc.vector.tensor_tensor(lam[:, 2, :], lam[:, 1, :], lam[:, 0, :], ALU.subtract))
                step(nc.vector.tensor_scalar(lam[:, 2, :], lam[:, 2, :], -0.8, None, ALU.add))
                wait_copied(dve, "rowsT")
                for i in range(2):
                    ins = nc.vector.tensor_scalar(wso[:, i, :], wso[:, i, :], cols[:, 5:6], 0.2, ALU.mult, ALU.mult)
                ins.then_inc(wso_ready, 1)

            def dproj(t):
                key = ("kd", t)
                wait_filled(dve, key)
                copied(make_qblk(kblk[:], bank(key)[:, 0:2 * P], 2 * BT), key)

            def dval(t):
                for i in range(2):
                    key = ("vd", t, i)
                    wait_filled(dve, key)
                    copied(nc.vector.tensor_tensor(vblk[:, 2 * i:2 * i + 2], bank(key).rearrange("p (b n d) -> p b n d", b=2, d=16),
                                                   broadcast(broadcast(maskv[:], 1, 2), 3, 16), ALU.mult), key)

            def halves(p):
                return sc[:, 2 * p:2 * p + 2, :].rearrange("p g (n k) -> p (g n) k", k=Q)

            def dsoft(t, p):
                dve.wait_ge(d_filled, 2 * t + 2)
                src = banks[:, side:side + 2, 2 * P * p:2 * P * p + 2 * P].rearrange("p g (n k) -> p g n k", k=Q)
                step(nc.vector.tensor_tensor(sc[:, 2 * p:2 * p + 2, :].rearrange("p g (n k) -> p g n k", k=Q), src,
                                             broadcast(broadcast(causal[:], 1, 2 * BT), 1, 2), ALU.add))
                step(nc.vector.tensor_reduce(small[:, 3 + p, :], halves(p), AX, ALU.max))
                nc.vector.tensor_tensor(halves(p), halves(p), broadcast(small[:, 3 + p, :], 2, Q), ALU.subtract).then_inc(d_sub, 1)

            def dprob(t, p):
                dve.wait_ge(d_exp, nth[("dprob", t, p)])
                r = small[:, 5 + p, :]
                step(nc.vector.tensor_reduce(r, halves(p), AX, ALU.add))
                step(nc.vector.reciprocal(r, r))
                r2 = r.rearrange("p (g m h s) -> p g m h s", g=2, m=2, h=2)[:, :, :, :, 1]
                step(nc.vector.tensor_tensor(r2, r2, lam[:, 2, :].rearrange("p (m g h) -> p g m h", m=2, g=G)[:, 2 * p:2 * p + 2], ALU.mult))
                step(nc.vector.tensor_tensor(halves(p), halves(p), broadcast(r, 2, Q), ALU.mult))
                both = sc[:, 2 * p:2 * p + 2, :].rearrange("p g (n s k) -> p (g n) s k", s=2, k=Q)
                nc.vector.tensor_tensor(attn[:, 2 * p:2 * p + 2, :].rearrange("p g (n k) -> p (g n) k", k=Q),
                                        both[:, :, 0, :], both[:, :, 1, :], ALU.add).then_inc(d_attn, 1)

            def drms(t):
                dve.wait_ge(d_sq, nth[("drms", t)])
                ms = small[:, 0, :]
                step(nc.vector.tensor_reduce(ms, view(sc, 0, 16, 16), AX, ALU.add))
                nc.vector.tensor_scalar(ms, ms, 1.0 / 16, LN_EPS, ALU.mult, ALU.add).then_inc(d_ms, 1)

            def doT(t):
                dve.wait_ge(d_rms, nth[("drms", t)])
                nc.vector.tensor_tensor(on.rearrange("p m (n d) -> p (m n) d", d=16), banks[:, side, 0:2 * P].rearrange("p (n d) -> p n d", d=16),
                                        broadcast(small[:, 0, :], 2, 16), ALU.mult).then_inc(d_on, 1)

            def gate(key):
                wait_filled(dve, key)
                nc.vector.tensor_reduce(small[:, 2, 0:1], bank(key)[:, 0:E], AX, ALU.max, negate=True).then_inc(g_max, 1)

            def best(key, bias):
                wait_copied(dve, key)
                step(nc.vector.reciprocal(small[:, 2, 2:3], small[:, 2, 1:2]))
                step(nc.vector.tensor_scalar(small[:, 1, 0:E], small[:, 1, 0:E], small[:, 2, 2:3], None, ALU.mult))
                ranked = small[:, 1, 0:E]
                if bias:
                    step(nc.vector.tensor_tensor(small[:, 7, 0:E], ranked, gb[:], ALU.add))
                    ranked = small[:, 7, 0:E]
                step(nc.vector.max(m8[:], ranked))
                step(nc.vector.max_index(ix[:], m8[:], ranked))
                step(nc.vector.tensor_copy(small[:, 8, 0:2], ix[:, 0:2]))
                step(nc.vector.tensor_scalar(small[:, 9, 0:E], iota8[:], small[:, 8, 0:1], None, ALU.is_equal))
                step(nc.vector.scalar_tensor_tensor(small[:, 10, 0:E], iota8[:], small[:, 8, 1:2], small[:, 9, 0:E], ALU.is_equal, ALU.add))
                ins = nc.vector.tensor_tensor(cw[:, 0:E], small[:, 10, 0:E], small[:, 1, 0:E], ALU.mult)
                if not bias:
                    step(ins)
                    step(nc.vector.tensor_reduce(small[:, 11, 0:1], cw[:, 0:E], AX, ALU.add))
                    step(nc.vector.reciprocal(small[:, 11, 1:2], small[:, 11, 0:1]))
                    ins = nc.vector.tensor_scalar(cw[:, 0:E], cw[:, 0:E], small[:, 11, 1:2], None, ALU.mult)
                ins.then_inc(cw_ready, 1)
                dve.wait_ge(cw_ready, gate_nth[key])

            def combine(key, t, e):
                wait_filled(dve, key)
                y, x = bank(key)[:, 0:P], x_sb[:, t, :]
                if e == E:
                    copied(nc.vector.tensor_tensor(x, y, x, ALU.add), key)
                else:
                    copied(nc.vector.scalar_tensor_tensor(x, y, cw[:, e:e + 1], x, ALU.mult, ALU.add), key)
                wait_copied(dve, key)

            def hid0(t, i):
                k, e = nth[("hid0", t, i)], (i + E) % NE0
                dve.wait_ge(h_act, k)
                if k > 2:
                    dve.wait_ge(l_ready, k - 2)
                    dve.wait_ge(tanh_ready, k - 2)
                h3 = banks[:, side + k % 2, 2 * P:].rearrange("p (r t) -> p r t", r=2)
                step(nc.vector.scalar_tensor_tensor(tmp[:, k % 2, 0, :], h3[:, 0, :], bcol[:, 0, NE0 + e:NE0 + e + 1],
                                                    hid[:, k % 2, 0, :], ALU.add, ALU.mult))
                nc.vector.scalar_tensor_tensor(tmp[:, k % 2, 1, :], h3[:, 1, :], bcol[:, 1, NE0 + e:NE0 + e + 1],
                                               hid[:, k % 2, 1, :], ALU.add, ALU.mult).then_inc(h_prod, 1)
                nc.vector.tensor_scalar(tmp[:, k % 2, 0, :], tmp[:, k % 2, 0, :], 7.0, None, ALU.min).then_inc(g_ready, 1)

            def act0(t, i):
                k = nth[("act0", t, i)]
                dve.wait_ge(g_ready, k)
                dve.wait_ge(l_ready, k)
                step(nc.vector.scalar_tensor_tensor(tmp[:, k % 2, 2, :], tmp[:, k % 2, 1, :], 1.0, tmp[:, k % 2, 0, :], ALU.add, ALU.mult))
                dve.wait_ge(tanh_ready, k)
                if i >= 2:
                    wait_filled(dve, ("y0", t, i - 2))
                elif t:
                    wait_filled(dve, ("y0", t - 1, NE0 - 2 + i))
                nc.vector.scalar_tensor_tensor(hid[:, k % 2, 3, :], hid[:, k % 2, 2, :], 1.0, tmp[:, k % 2, 2, :],
                                               ALU.add, ALU.mult).then_inc(a_ready, 1)

            def lat_(t):
                dve.wait_ge(ln_rstd, 1 + nth[("ln", 4, t)])
                step(normalised(lat[:, t, :], xln[:, t, :], 34 + t))
                step(nc.vector.tensor_tensor(lat[:, t, :], lat[:, t, :], bc[:, 4, :], ALU.mult))
                nc.vector.tensor_tensor(lat[:, t, :], lat[:, t, :], bc[:, 5, :], ALU.add).then_inc(ln_done, 1)

            def qk_(t, n):
                if n % 2:
                    copy_job(("qk", t, n), qk[t][:, :, n // 2 * 8 + n % 2:n // 2 * 8 + 8:2, :].rearrange("p b h q -> p h b q"),
                             bank(("qk", t, n)).rearrange("p (h b q) -> p h b q", h=4, b=BT))

            def oT1(t, n):
                if n == 1:
                    copy_job(("oT1", t, n), oT[:, 4 * n:4 * n + 4, :].rearrange("p i t -> p (i t)"), bank(("oT1", t, n)))

            def out1(t):
                dve.wait_ge(bias_added, 2 + t)
                add_to_x(("out1", t), t, xb_sb[:, t, :])

            def lin(t):
                kp, ic = keep[:].rearrange("p b q -> p (b q)"), icnt[:].rearrange("p b q -> p (b q)")
                ac, z = ("ac", t), ("z", t)
                nc.vector.memset(scan[64:65, 0, :], 1.0)
                wait_filled(dve, z)
                step(nc.vector.tensor_tensor_scan(scan[32:64, 1, :], kp[32:64], bank(z)[32:64, 0:P], 0.0, ALU.mult, ALU.add))
                wait_filled(dve, ac)
                step(nc.vector.tensor_tensor_scan(scan_c, kp, bank(ac)[0:64, P:2 * P], 0.0, ALU.mult, ALU.add))
                copied(nc.vector.tensor_tensor(scan[32:64, 1, :], scan[32:64, 1, :], ic[32:64], ALU.mult), z)
                wait_copied(dve, z)
                copied(nc.vector.tensor_tensor(scan[0:64, 0, :], bank(ac)[0:64, 0:P], scan_c, ALU.mult), ac)
                wait_copied(dve, ac)
                step(nc.vector.tensor_tensor(scan[32:64, 0, :], scan[32:64, 0, :], scan[32:64, 1, :], ALU.mult))
                nc.vector.tensor_tensor(scan[0:64, 0, :], scan[0:64, 0, :], ic, ALU.mult).then_inc(pr_ready, 1)

            def hid1(t, e):
                if e % 2 == 0:
                    return
                dve.wait_ge(h1_filled, nth[("hid1", t, e)])
                if e >= 2:
                    wait_filled(dve, ("y1", t, e - 2))
                elif t:
                    wait_filled(dve, ("y1", t - 1, E - 2 + e))
                for k in range(KH):
                    ins = nc.vector.tensor_scalar(hid[:, e % 2, k, :], banks[:, side + e % 2, P * k:P * k + P],
                                                  cols[:, 22 + KH * e + k:23 + KH * e + k], 0.0, ALU.add, ALU.max)
                ins.then_inc(h1_odd, 1)

            def b1(t):
                wait_filled(dve, ("b1", t))
                copied(nc.vector.tensor_tensor(x_sb[:, t, :], bank(("b1", t))[:, 0:P], x_sb[:, t, :], ALU.add), ("b1", t))

            parts = {"start": start, "lam_dots": lam_dots, "lam_end": lam_end, "prep": prep, "cstat": cstat, "weight": weight, "scores0": scores0, "scores1": scores1, "lat1": lat1,
                     "norm0": lambda b: invert_sums(tile0(b, 0)), "norm1": lambda b: invert_sums(tile1(b, 0)),
                     "attend0": attend0, "attend1": attend1, "heads0": heads0, "out0": out0, "ln": ln, "xT": xT_, "dproj": dproj, "dval": dval,
                     "dsoft": dsoft, "dprob": dprob, "drms": drms, "doT": doT,
                     "dout": lambda t: add_to_x(("dout", t), t, x_sb[:, t, :]),
                     "gate0": lambda t: gate(("gate0", t)), "gate1": lambda t: gate(("gate1", t)),
                     "best0": lambda t: best(("gate0", t), True), "best1": lambda t: best(("gate1", t), False),
                     "hid0": hid0, "act0": act0, "y0": lambda t, i: combine(("y0", t, i), t, (i + E) % NE0),
                     "lat": lat_, "qk": qk_, "oT1": oT1, "out1": out1, "lin": lin,
                     "linout": lambda t: add_to_x(("linout", t), t, x_sb[:, t, :]),
                     "hid1": hid1, "y1": lambda t, e: combine(("y1", t, e), t, e), "b1": b1}
            gate_nth = {key: i + 1 for i, key in enumerate(k for k in ORDER if k[0] in ("gate0", "gate1"))}
            for kind, *a in order(DVE):
                if kind in parts:
                    parts[kind](*a)

        @block.tensor
        def _(pe):
            def mm(dst, lhsT, rhs, start=True, stop=True, at=None):
                return nc.tensor.matmul(dst, lhsT, rhs, start=start, stop=stop, tile_position=at)

            def tr(dst, src):
                k = src.shape[0]
                return nc.tensor.transpose(dst, src, ident[0:k, 0:k])

            def start():
                pe.wait_ge(ident_ready, 1)
                pe.wait_ge(w0_loaded, 48)
                for i in range(3):
                    ins = tr(bank("w0T")[:, P * i:P * i + P], w0raw[:, i, :])
                filled(ins, "w0T")
                pe.wait_ge(b0_loaded, 48)
                filled(tr(bank("b0T")[:, 0:3], rows[0:3, :]), "b0T")
                pe.wait_ge(ln_done, 1)
                key = ("xT", 0, 0)
                wait_bank_free(pe, key)
                for t in range(NT):
                    ins = tr(bank(key)[:, P * t:P * t + P], xln[:, t, :])
                filled(ins, key)
                wait_copied(pe, key)
                wait_bank_free(pe, "q0T")
                filled(mm(bank("q0T")[:, 0:T], w0T[:, 0, :], xT[:]), "q0T")

            def rows_():
                pe.wait_ge(rows_loaded, 16 * 11)
                for key in ("rowsT", "bias0T", "w0oT"):
                    wait_bank_free(pe, key)
                    if key == "rowsT":
                        ins = tr(bank(key)[:, 0:ROWS], rows)
                    if key == "bias0T":
                        for r in range(2):
                            ins = tr(bank(key)[:, 2 * NE0 * r:2 * NE0 * r + 2 * NE0], brow.rearrange("n (i r) -> n r i", r=2)[:, r, :])
                    if key == "w0oT":
                        ins = tr(bank(key)[:, 0:D], w0raw[:, 3, :])
                    filled(ins, key)

            def prep(b, k):
                key = (("ctxT", "k0T", "v0")[k], b)
                if k == 0:
                    pe.wait_ge(ctx_loaded[b], 16)
                    wait_bank_free(pe, key)
                    for c in range(C):
                        ins = tr(bank(key)[:, P * c:P * c + P], ctx_sb[:, b, c, :])
                if k == 1:
                    wait_copied(pe, ("ctxT", b))
                    wait_bank_free(pe, key)
                    ins = mm(bank(key), w0T[:, 1, :], ctxT[:, b % CT, :])
                if k == 2:
                    wait_bank_free(pe, key)
                    for c in range(C):
                        ins = mm(bank(key)[:, P * c:P * c + P], ctxT[:, b % CT, P * c:P * c + P], w0T[:, 2, :])
                filled(ins, key)

            raw_nth = {("w11T", e): e for e in range(E)} | {("w12T", e): E + e for e in range(E)}

            def weight(what, e):
                key = ("weight", what, e)
                wait_bank_free(pe, key)
                bk = bank(key)
                if what == "w13T":
                    pe.wait_ge(exp0_loaded[e // 4 % 2], 16 * (2 if 4 <= e < E else 4))
                    for w in range(2):
                        for r in range(2):
                            src = shared_raw[:, 2 * w + r, :] if e == E else w1raw0[:, w, 2 * e + r, :]
                            ins = tr(bk[:, P * (2 * w + r):P * (2 * w + r + 1)], src)
                if what == "w2T":
                    pe.wait_ge(exp0_w2_loaded, 16 * 2)
                    for m in range(min(4, NE0 - 4 * e)):
                        ins = tr(bk[:, P * m:P * m + P], w2raw[:, 4 * e + m, :])
                if what == "m12":
                    pe.wait_ge(lin_loaded, 16 * 10)
                    mm(bk[:, 0:64], wl[:, 0, :], lowr[:, 0:2, :].rearrange("p a r -> p (a r)"))
                    ins = mm(bk[:, 64:128], wl[:, 1, :], lowr[:, 2:4, :].rearrange("p a r -> p (a r)"))
                if what == "woT":
                    ins = tr(bk[:, 0:P], wl[:, 2, :])
                if what == "g":
                    pe.wait_ge(uu_ready, 1)
                    wait_copied(pe, ("weight", "woT", 0))
                    ins = mm(bk[0:65, 0:P], uu[:], woT[:])
                if what == "wkT":
                    pe.wait_ge(wkv_loaded, 16)
                    for m in range(4):
                        ins = tr(bk[:, P * m:P * m + P], wkv1[:, P * (4 * e + m):P * (4 * e + m + 1)])
                if what in ("w11T", "w12T"):
                    i = raw_nth[what, e]
                    pe.wait_ge(exp1_loaded[i % RAW_SLOTS], 16 * (i // RAW_SLOTS + 1))
                    for k in range(KH):
                        ins = tr(bk[:, P * k:P * k + P], wraw1[:, i % RAW_SLOTS, k, :])
                filled(ins, key)

            def scores0(b, g):
                k = tile0(b, g)
                if k == 0:
                    pe.wait_ge(qblk_ready, 1)
                if g == 0:
                    wait_copied(pe, ("k0T", b))
                if k >= 2:
                    pe.wait_ge(s_exp, k - 1)
                r = slice(32 * g, 32 * g + 32)
                mm(banks[:, g % 2, :], qblk[r, b].rearrange("p j q -> p (j q)"), k0T[r, b % KV, :], at=(32 * g, 0)).then_inc(s_filled, 1)

            def attend0(b, c):
                if c < C:
                    key = ("p0T", b, c)
                    if c == 0:
                        pe.wait_ge(p_ready, tile0(b, G))
                    wait_bank_free(pe, key)
                    for g in range(G):
                        ins = tr(bank(key)[:, P * g:P * g + P], big[:, (b % 2) * G + g, P * c:P * c + P])
                    filled(ins, key)
                c -= 1
                if c < 0:
                    return
                wait_copied(pe, ("p0T", b, c))
                if c == 0:
                    wait_copied(pe, ("v0", b))
                    if b == BT:
                        pe.wait_ge(o0T_ready, 1)
                for g in range(G):
                    ins = mm(acc[32 * g:32 * g + 32, P * (b % BT):P * (b % BT) + P], v0[:, b % KV, c, 32 * g:32 * g + 32],
                             pT[:, c, P * g:P * g + P], start=c == 0, stop=c == C - 1, at=(0, 32 * g))
                ins.then_inc(av_read, 1)

            def project(key, n_in, lhs, rhs):
                wait_bank_free(pe, key)
                for k in range(n_in):
                    ins = mm(bank(key)[:, 0:P], lhs(k), rhs(k), start=k == 0, stop=k == n_in - 1)
                filled(ins, key)

            def out0(t):
                pe.wait_ge(o0T_ready, t + 1)
                project(("out0", t), 1, lambda k: o0T, lambda k: w0T[:, 3, :])

            def transposed(key, src, done):
                pe.wait_ge(ln_done, done)
                wait_bank_free(pe, key)
                filled(tr(bank(key)[:, 0:P], src), key)

            def xT_(k, t):
                transposed(("xT", k, t), xln[:, t, :], done_nth["xT", k, t])

            def dproj(t):
                pe.wait_ge(self_loaded, 16 * 8)
                wait_copied(pe, ("xT", 1, t))
                for key, w in ((("qd", t), 0), (("kd", t), 1)):
                    wait_bank_free(pe, key)
                    for m in range(2):
                        ins = mm(bank(key)[:, P * m:P * m + P], ws[:, w, P * m:P * m + P], xT[:, P * t:P * t + P])
                    filled(ins, key)

            def dval(t):
                for i in range(2):
                    key = ("vd", t, i)
                    wait_bank_free(pe, key)
                    for m in range(2):
                        ins = mm(bank(key)[:, T * m:T * m + T], x_rep[:, 2 * i + m].rearrange("p j q -> p (j q)"), ws[:, 2, :])
                    filled(ins, key)

            def dscore(t):
                wait_copied(pe, ("qd", t))
                wait_copied(pe, ("kd", t))
                if t:
                    pe.wait_ge(h_prod, NE0 * t)
                for p in range(2):
                    if p:
                        pe.wait_ge(d_filled, 2 * t + 1)
                    for g in (2 * p, 2 * p + 1):
                        r = slice(32 * g, 32 * g + 32)
                        for m in range(2):
                            for b in range(BT):
                                q = slice(Q * b, Q * b + Q)
                                col = 2 * P * p + P * m
                                ins = mm(banks[q, side + g % 2, col:col + P], qdT[r, m, q],
                                         kblk[r, m * BT + b].rearrange("p j k -> p (j k)"), at=(32 * g, Q * b))
                    ins.then_inc(d_filled, 1)

            def daT(t):
                key = ("daT", t)
                pe.wait_ge(d_attn, 2 * t + 2)
                wait_bank_free(pe, key)
                for g in range(G):
                    ins = tr(bank(key)[:, P * g:P * g + P], attn[:, g, :])
                filled(ins, key)

            def dpv(t):
                wait_copied(pe, ("daT", t))
                wait_copied(pe, ("vd", t, 1))
                for g in range(G):
                    for b in range(BT):
                        r = slice(Q * b, Q * b + Q)
                        ins = mm(banks[r, side, 0:2 * P].rearrange("p (m g d) -> p m g d", m=2, g=G)[:, :, g, :], attnT[:, g, r],
                                 vblk[:, b].rearrange("p (m g h) d -> p m g (h d)", m=2, g=G)[:, :, g, :], at=(0, Q * b))
                ins.then_inc(d_out, 1)

            def doT(t):
                pe.wait_ge(d_on, t + 1)
                key = ("doT", t)
                wait_bank_free(pe, key)
                for m in range(2):
                    ins = tr(bank(key)[:, P * m:P * m + P], on[:, m, :])
                filled(ins, key)

            def dout(t):
                wait_copied(pe, ("doT", t))
                pe.wait_ge(wso_ready, 1)
                project(("dout", t), 2, lambda k: odT[:, k, :], lambda k: wso[:, k, :])

            def gate(key, k, c0):
                t = key[1]
                wait_copied(pe, ("xT", k, t))
                wait_bank_free(pe, key)
                filled(mm(bank(key)[:, 0:E], xT[:, P * t:P * t + P], cols[:, c0:c0 + E]), key)

            def cwT_(layer, t):
                key = (f"cwT{layer}", t)
                pe.wait_ge(cw_ready, gate_nth[f"gate{layer}", t])
                wait_bank_free(pe, key)
                filled(tr(bank(key)[0:NE0, 0:P], cw[:]), key)

            def hid0(t, i):
                k, e = nth[("hid0", t, i)], (i + E) % NE0
                wait_copied(pe, ("xT", 2, t))
                if k > 2:
                    pe.wait_ge(h_prod, k - 2)
                for w in range(2):
                    for r in range(2):
                        ins = mm(banks[:, side + k % 2, P * (2 * w + r):P * (2 * w + r + 1)], w13T[:, e, 2 * w + r, :], xT[:, P * t:P * t + P])
                ins.then_inc(h_filled, 1)

            def y0(t, i):
                k, e = nth[("act0", t, i)], (i + E) % NE0
                key = ("y0", t, i)
                pe.wait_ge(a_ready, k)
                wait_bank_free(pe, key)
                ins = mm(bank(key)[:, 0:P], hid[:, k % 2, 3, :], w2T[:, e, :], stop=e != E)
                if e == E:
                    wait_copied(pe, ("cwT0", t))
                    pe.wait_ge(b2_loaded, 48)
                    ins = mm(bank(key)[:, 0:P], cwT[:], b2x[:], start=False)
                filled(ins, key)

            def lat_(t):
                transposed(("lat", t), lat[:, t, :], done_nth["lat", t])

            def q1(t, n):
                key = ("q1", t, n)
                wait_copied(pe, ("lat", t))
                pe.wait_ge(wq1_loaded, 32)
                wait_bank_free(pe, key)
                for m in range(4):
                    ins = mm(bank(key)[:, P * m:P * m + P], wq1[:, P * (4 * n + m):P * (4 * n + m + 1)], latT[:, P * t:P * t + P])
                filled(ins, key)

            def qk_(t, n):
                a, m = n // 2, n % 2
                key = ("qk", t, n)
                wait_copied(pe, ("q1", t, a))
                wait_bank_free(pe, key)
                r = slice(HALF_H * m, HALF_H * m + HALF_H)
                for j in range(4):
                    ins = mm(bank(key)[:, P * j:P * j + P], wkT[r, 4 * a + j, :], q1T[r, 4 * a + j, :], at=(HALF_H * m, 0))
                filled(ins, key)

            def xnT_(b):
                key = ("xnT", b)
                pe.wait_ge(xn_ready, b + 1)
                wait_bank_free(pe, key)
                for c in range(C):
                    ins = tr(bank(key)[:, P * c:P * c + P], ctx_sb[:, b, c, :])
                filled(ins, key)

            def queries1(b, g):
                return qk[b // BT][:, b % BT, HG * g:HG * g + HG, :].rearrange("p h q -> p (h q)")

            def lat1(b):
                key = ("lat1", b)
                if b % BT == 0:
                    for m in range(4):
                        wait_copied(pe, ("qk", b // BT, m))
                wait_bank_free(pe, key)
                for g in range(G):
                    ins = mm(bank(key)[:, Q * g:Q * g + Q], queries1(b, g), latT[:, Q * b:Q * b + Q])
                filled(ins, key)

            def scores1(b, g):
                k = tile1(b, g)
                if g == 0:
                    wait_copied(pe, ("xnT", b))
                pe.wait_ge(s_max, k - 1)
                mm(banks[:, g % 2, :], queries1(b, g), xnT[:, b % CT, :]).then_inc(s_filled, 1)

            def attend1(b, c):
                if c <= C:
                    key = ("p1T", b, c)
                    if c == 0:
                        pe.wait_ge(p_ready, tile1(b, G))
                    wait_bank_free(pe, key)
                    m = P if c < C else Q
                    for g in range(G):
                        ins = tr(bank(key)[0:m, P * g:P * g + P], big[:, (b % 2) * G + g, P * c:P * c + m])
                    filled(ins, key)
                c -= 1
                if c < 0:
                    return
                wait_copied(pe, ("p1T", b, c))
                if c == 0 and b:
                    pe.wait_ge(acc_read, b)
                if c < C:
                    ins = mm(acc, ctx_sb[:, b, c, :], pT[:, c, :], start=c == 0, stop=False)
                else:
                    r = slice(Q * (b % BT), Q * (b % BT) + Q)
                    ins = mm(acc, lat[r, b // BT, :], pT[r, c, :], start=False, at=(Q * (b % BT), 0))
                ins.then_inc(av_read, 1)

            def oT1(t, n):
                key = ("oT1", t, n)
                pe.wait_ge(acc_read, BT * (t + 1))
                wait_bank_free(pe, key)
                for m in range(4):
                    for h in range(2):
                        head = 2 * (4 * n + m) + h
                        ins = mm(bank(key)[HALF_H * h:HALF_H * h + HALF_H, P * m:P * m + P],
                                 wkv1[:, HALF_H * (16 + head):HALF_H * (17 + head)], yT[:, head, :], at=(0, HALF_H * h))
                filled(ins, key)

            def out1(t):
                for n in range(2):
                    wait_copied(pe, ("oT1", t, n))
                project(("out1", t), 8, lambda k: oT[:, k, :], lambda k: wout1[:, k, :])

            def lin(t):
                x5 = xT[:, P * t:P * t + P]
                wait_copied(pe, ("xT", 5, t))
                wait_bank_free(pe, ("ac", t))
                mm(bank(("ac", t))[0:64, 0:P], m12[:, 0:64], x5)
                filled(mm(bank(("ac", t))[0:64, P:2 * P], m12[:, 64:128], x5), ("ac", t))
                wait_bank_free(pe, ("z", t))
                filled(mm(bank(("z", t))[32:64, 0:P], lowr[:, 4, :], x5, at=(0, 32)), ("z", t))

            def linout(t):
                pe.wait_ge(pr_ready, nth[("lin", t)])
                project(("linout", t), 1, lambda k: scan[:, 0, :], lambda k: gl[:])

            def hid1(t, e):
                k = nth[("hid1", t, e)]
                wait_copied(pe, ("xT", 6, t))
                if k > 2:
                    pe.wait_ge(h1_odd if e % 2 else h1_even, (k - 1) // 2)
                for m in range(KH):
                    ins = mm(banks[:, side + e % 2, P * m:P * m + P], w11T[:, e, m, :], xT[:, P * t:P * t + P])
                ins.then_inc(h1_filled, 1)

            def y1(t, e):
                k = nth[("hid1", t, e)]
                pe.wait_ge(h1_odd if e % 2 else h1_even, (k + 1) // 2)
                project(("y1", t, e), KH, lambda m: hid[:, e % 2, m, :], lambda m: w12T[:, e, m, :])

            def b1(t):
                wait_copied(pe, ("cwT1", t))
                project(("b1", t), 1, lambda k: cwT[0:E, :], lambda k: b2y[:])

            parts = {"start": start, "rows": rows_, "prep": prep, "weight": weight, "scores0": scores0, "attend0": attend0, "out0": out0, "xT": xT_,
                     "dproj": dproj, "dval": dval, "dscore": dscore, "daT": daT, "dpv": dpv, "doT": doT, "dout": dout,
                     "gate0": lambda t: gate(("gate0", t), 2, 6), "gate1": lambda t: gate(("gate1", t), 6, 14),
                     "cwT0": lambda t: cwT_(0, t), "cwT1": lambda t: cwT_(1, t), "hid0": hid0, "y0": y0, "lat": lat_, "q1": q1,
                     "qk": qk_, "xnT": xnT_, "lat1": lat1, "scores1": scores1, "attend1": attend1, "oT1": oT1, "out1": out1,
                     "lin": lin, "linout": linout, "hid1": hid1, "y1": y1, "b1": b1}
            gate_nth = {key: i + 1 for i, key in enumerate(k for k in ORDER if k[0] in ("gate0", "gate1"))}
            done_nth = {key: i + 2 for i, key in enumerate(k for k in order(DVE) if k[0] in ("xT", "lat"))}
            for kind, *a in ORDER:
                if kind in parts:
                    parts[kind](*a)


def kernel(**inputs):
    import concourse.bacc as bacc
    from concourse.bass_utils import run_bass_kernel_spmd

    nc = bacc.Bacc("TRN2", target_bir_lowering=False, num_devices=1)
    arrays, d = {}, {}
    for name, value in inputs.items():
        a = np.ascontiguousarray(value)
        if a.ndim == 0:
            a = a.reshape(1)
        arrays["in_" + name] = a
        d[name] = nc.dram_tensor("in_" + name, a.shape, mybir.dt.from_np(a.dtype), kind="ExternalInput").ap()
    out = nc.dram_tensor("out_x", (B, Q, D), F32, kind="ExternalOutput").ap()
    build(nc, d, out)
    result = run_bass_kernel_spmd(nc, [arrays], core_ids=[0])
    return result.results[0]["out_x"]
```
